# Optimizing a Trainium2 kernel written in Bass

```python
import numpy as np
import jax
import jax.numpy as jnp

def _softmax(x, axis=-1):
    return jax.nn.softmax(x, axis=axis)

def _gelu(x):
    return jax.nn.gelu(x, approximate=True)

def _silu(x):
    return jax.nn.silu(x)

def _sigmoid(x):
    return jax.nn.sigmoid(x)

def _layernorm(x, axis=-1, eps=1e-05):
    m = jnp.mean(x, axis=axis, keepdims=True)
    v = jnp.var(x, axis=axis, keepdims=True)
    return (x - m) / jnp.sqrt(v + eps)

def _scatter_add(tgt, idx, src, axis=0):
    return tgt.at[idx].add(src)

def _segment_sum(src, seg, n):
    return jax.ops.segment_sum(src, seg, n)
kernel_name = 'mk_macaron_d1_jaxref_r8_437e75'

def setup_inputs(seed: int=0):
    np.random.seed(seed)
    _w = jnp.asarray

    def _L0_attn_setup():
        import jax, jax.numpy as jnp
        import numpy as np
        B, S, D = (2, 256, 128)
        N_HEADS, N_KV_HEADS = (16, 4)
        HEAD_DIM = D // N_HEADS
        KV_GROUPS = N_HEADS // N_KV_HEADS
        ROPE_BASE = 10000.0

        def _apply_rope(t, cos, sin):
            t1, t2 = jnp.split(t, 2, axis=-1)
            return jnp.concatenate([t1 * cos - t2 * sin, t1 * sin + t2 * cos], axis=-1)
        key = jax.random.key(seed)
        ks = jax.random.split(key, 5)
        s = 0.02
        return {'x': jax.random.normal(ks[0], (B, S, D), dtype=jnp.float32), 'wq': jax.random.normal(ks[1], (D, D), dtype=jnp.float32) * s, 'wk': jax.random.normal(ks[2], (D, N_KV_HEADS * HEAD_DIM), dtype=jnp.float32) * s, 'wv': jax.random.normal(ks[3], (D, N_KV_HEADS * HEAD_DIM), dtype=jnp.float32) * s, 'wo': jax.random.normal(ks[4], (D, D), dtype=jnp.float32) * s}
    _L0_attn_in = _L0_attn_setup()

    def _L0_ffn_setup():
        import jax, jax.numpy as jnp
        import numpy as np
        B, N, D, E, MULT = (4, 256, 128, 8, 4)
        F = D * MULT

        def _top2_gate(xn, Wg):
            logits = jnp.einsum('bnd,ed->bne', xn, Wg)
            probs = jax.nn.softmax(logits, axis=-1)
            top1 = jnp.argmax(probs, axis=-1)
            t1v = jnp.take_along_axis(probs, top1[..., None], axis=-1)[..., 0]
            masked = jnp.where(jax.nn.one_hot(top1, probs.shape[-1], dtype=bool), -jnp.inf, probs)
            top2 = jnp.argmax(masked, axis=-1)
            t2v = jnp.take_along_axis(masked, top2[..., None], axis=-1)[..., 0]
            denom = t1v + t2v + 1e-09
            combine = jnp.stack([t1v / denom, t2v / denom], axis=-1)
            idx = jnp.stack([top1, top2], axis=-1)
            return (combine, idx)
        key = jax.random.key(seed)
        ks = jax.random.split(key, 8)
        s_in = 1.0 / np.sqrt(D)
        s_hid = 1.0 / np.sqrt(F)
        return {'x': jax.random.normal(ks[0], (B, N, D), dtype=jnp.float32), 'gamma': jnp.ones((D,), dtype=jnp.float32), 'beta': jnp.zeros((D,), dtype=jnp.float32), 'Wg': jax.random.normal(ks[1], (E, D), dtype=jnp.float32) * s_in, 'W1': jax.random.normal(ks[2], (E, D, F), dtype=jnp.float32) * s_in, 'b1': jax.random.normal(ks[3], (E, F), dtype=jnp.float32) * 0.01, 'W2': jax.random.normal(ks[4], (E, F, D), dtype=jnp.float32) * s_hid, 'b2': jax.random.normal(ks[5], (E, D), dtype=jnp.float32) * 0.01}
    _L0_ffn_in = _L0_ffn_setup()
    _d = {'L0_attn_x': _L0_attn_in['x'], 'L0_attn_wq': _L0_attn_in['wq'], 'L0_attn_wk': _L0_attn_in['wk'], 'L0_attn_wv': _L0_attn_in['wv'], 'L0_attn_wo': _L0_attn_in['wo'], 'L0_ffn_gamma': _L0_ffn_in['gamma'], 'L0_ffn_beta': _L0_ffn_in['beta'], 'L0_ffn_Wg': _L0_ffn_in['Wg'], 'L0_ffn_W1': _L0_ffn_in['W1'], 'L0_ffn_b1': _L0_ffn_in['b1'], 'L0_ffn_W2': _L0_ffn_in['W2'], 'L0_ffn_b2': _L0_ffn_in['b2']}
    _x0 = _d['L0_attn_x']
    _d['L0_attn_x'] = jax.random.normal(jax.random.fold_in(jax.random.key(seed), 1), (8, 512, 128), dtype=_x0.dtype)
    del _x0
    return _d

def reference(L0_attn_x, L0_attn_wq, L0_attn_wk, L0_attn_wv, L0_attn_wo, L0_ffn_gamma, L0_ffn_beta, L0_ffn_Wg, L0_ffn_W1, L0_ffn_b1, L0_ffn_W2, L0_ffn_b2):

    def _L0_attn_ref(x, wq, wk, wv, wo):
        import jax, jax.numpy as jnp
        import numpy as np
        B, S, D = (2, 256, 128)
        N_HEADS, N_KV_HEADS = (16, 4)
        HEAD_DIM = D // N_HEADS
        KV_GROUPS = N_HEADS // N_KV_HEADS
        ROPE_BASE = 10000.0

        def _apply_rope(t, cos, sin):
            t1, t2 = jnp.split(t, 2, axis=-1)
            return jnp.concatenate([t1 * cos - t2 * sin, t1 * sin + t2 * cos], axis=-1)
        Bx, Sx, Dx = x.shape
        q = (x @ wq).reshape(Bx, Sx, N_HEADS, HEAD_DIM)
        k = (x @ wk).reshape(Bx, Sx, N_KV_HEADS, HEAD_DIM)
        v = (x @ wv).reshape(Bx, Sx, N_KV_HEADS, HEAD_DIM)
        half = HEAD_DIM // 2
        inv_freq = 1.0 / ROPE_BASE ** (jnp.arange(0, half, dtype=jnp.float32) / half)
        pos = jnp.arange(Sx, dtype=jnp.float32)
        ang = pos[:, None] * inv_freq[None, :]
        cos = jnp.cos(ang)[:, None, :]
        sin = jnp.sin(ang)[:, None, :]
        q = _apply_rope(q, cos, sin)
        k = _apply_rope(k, cos, sin)
        k = jnp.broadcast_to(k[:, :, None, :, :], (Bx, Sx, KV_GROUPS, N_KV_HEADS, HEAD_DIM)).reshape(Bx, Sx, N_HEADS, HEAD_DIM)
        v = jnp.broadcast_to(v[:, :, None, :, :], (Bx, Sx, KV_GROUPS, N_KV_HEADS, HEAD_DIM)).reshape(Bx, Sx, N_HEADS, HEAD_DIM)
        scale = 1.0 / jnp.sqrt(jnp.float32(HEAD_DIM))
        scores = jnp.einsum('bshd,bthd->bhst', q, k) * scale
        causal = jnp.tril(jnp.ones((Sx, Sx), dtype=bool))
        scores = jnp.where(causal[None, None, :, :], scores, jnp.float32(-jnp.inf))
        attn = jax.nn.softmax(scores, axis=-1)
        out = jnp.einsum('bhst,bthd->bshd', attn, v).reshape(Bx, Sx, Dx)
        return out @ wo

    def _L0_ffn_ref(x, gamma, beta, Wg, W1, b1, W2, b2):
        import jax, jax.numpy as jnp
        import numpy as np
        B, N, D, E, MULT = (4, 256, 128, 8, 4)
        F = D * MULT

        def _top2_gate(xn, Wg):
            logits = jnp.einsum('bnd,ed->bne', xn, Wg)
            probs = jax.nn.softmax(logits, axis=-1)
            top1 = jnp.argmax(probs, axis=-1)
            t1v = jnp.take_along_axis(probs, top1[..., None], axis=-1)[..., 0]
            masked = jnp.where(jax.nn.one_hot(top1, probs.shape[-1], dtype=bool), -jnp.inf, probs)
            top2 = jnp.argmax(masked, axis=-1)
            t2v = jnp.take_along_axis(masked, top2[..., None], axis=-1)[..., 0]
            denom = t1v + t2v + 1e-09
            combine = jnp.stack([t1v / denom, t2v / denom], axis=-1)
            idx = jnp.stack([top1, top2], axis=-1)
            return (combine, idx)
        residual = x
        mu = jnp.mean(x, axis=-1, keepdims=True)
        var = jnp.mean(jnp.square(x - mu), axis=-1, keepdims=True)
        xn = (x - mu) / jnp.sqrt(var + 1e-05) * gamma + beta
        combine, idx = _top2_gate(xn, Wg)
        n_expert = Wg.shape[0]
        onehot = jax.nn.one_hot(idx, n_expert, dtype=x.dtype)
        gates = jnp.einsum('bns,bnse->ebn', combine, onehot)

        def body(acc, params):
            w1, b1e, w2, b2e, g = params
            h = jax.nn.gelu(jnp.einsum('bnd,df->bnf', xn, w1) + b1e, approximate=True)
            y = jnp.einsum('bnf,fd->bnd', h, w2) + b2e
            return (acc + g[..., None] * y, None)
        out, _ = jax.lax.scan(body, jnp.zeros_like(x), (W1, b1, W2, b2, gates))
        return residual + out
    x = L0_attn_x
    x = x + 0.5 * _L0_ffn_ref(_layernorm(x, axis=-1), L0_ffn_gamma, L0_ffn_beta, L0_ffn_Wg, L0_ffn_W1, L0_ffn_b1, L0_ffn_W2, L0_ffn_b2)
    x = x + _L0_attn_ref(_layernorm(x, axis=-1), L0_attn_wq, L0_attn_wk, L0_attn_wv, L0_attn_wo)
    x = x + 0.5 * _L0_ffn_ref(_layernorm(x, axis=-1), L0_ffn_gamma, L0_ffn_beta, L0_ffn_Wg, L0_ffn_W1, L0_ffn_b1, L0_ffn_W2, L0_ffn_b2)
    return x

_drawn_inputs = setup_inputs


def setup_inputs(seed=0):
    import zlib

    import numpy as np

    out = dict(_drawn_inputs(seed))
    spreads = {'L0_ffn_gamma': (1.0, 0.2), 'L0_ffn_beta': (0.0, 0.1)}
    factors = {'L0_attn_wq': 8.0,
     'L0_attn_wk': 8.0,
     'L0_attn_wv': 8.0,
     'L0_attn_wo': 8.0,
     'L0_ffn_b1': 8.0,
     'L0_ffn_b2': 8.0}
    for name, (base, spread) in spreads.items():
        noise = np.random.default_rng([zlib.crc32(name.encode()), seed]).standard_normal(out[name].shape)
        drawn = base * np.exp(spread * noise) if base else spread * noise
        out[name] = jnp.asarray(drawn.astype(out[name].dtype))
    for name, factor in factors.items():
        out[name] = (out[name] * factor).astype(out[name].dtype)
    return out
```

```python
from contextlib import ExitStack

import numpy as np

import concourse.bass as bass
from concourse import mybir

F32 = mybir.dt.float32
F32R = mybir.dt.float32r
BF16 = mybir.dt.bfloat16
ALU = mybir.AluOpType
ACT = mybir.ActivationFunctionType
AX_X = mybir.AxisListType.X

P = 128
SEQS, S, D = 8, 512, 128
TILES = S // P
EXPERTS, F = 8, 512
CHUNKS = F // P
HEADS, KV, HD = 16, 4, 8
GROUPS = HEADS // KV
HALF = HD // 2
ROPED = HEADS + KV
SLOT = P // KV
QK = ROPED * HD
QKV = QK + KV * HD
STACK = 3 * HD
EPS = 1e-5
GATE_EPS = 1e-9
MASKED = -1e30
SCALE = float(1.0 / np.sqrt(np.float32(HD)))

FFN_CHUNKS = EXPERTS * CHUNKS
LAG = 3
TURNS = SEQS - 1

UP_BANK, Y_BANK, PV_BANK, GATE_BANK, MISC_BANK = 0, 2, 4, 5, 7
SCORE_BANK, MAX_BANK = 0, 5

MAX_BLOCKS = [(kv, tiles) for kv in range(KV) for tiles in ([(3, 0)], [(0, 0), (2, P)], [(1, 0)])]
NMAX = len(MAX_BLOCKS)

FFN_PREP = ["zT", "logits", "gT"]
ATT_PREP = ["nT", "qkv0", "qkv1", "kT", "qT0", "qT1", "qT2", "qT3"]
ATTEND = ["q2T0", "q2T1", "zT:0", "q2T2", "uT0", "logits:0", "q2T3", "uT1", "uT2", "gT:0"]
ATTEND_END = ["uT3", "aT", "y"]
MISC_FIRST = ["zT:0", "logits:0", "gT:0", "fin:0"] + ATT_PREP
MISC_TURN = ATTEND + ATTEND_END + ["zT:1", "logits:1", "gT:1", "fin:0"] + ATT_PREP + ["fin:1"]
MISC_LAST = [x for x in ATTEND if ":" not in x] + ATTEND_END + ["zT:1", "logits:1", "gT:1", "fin:1"]

AT = {"copy_u3": 0, "uT3": 1, "norm3": 1, "aT": 4, "y": 6, "stats:1": 6, "z:1": 10, "zT:1": 12,
      "xlo:1": 12, "logits:1": 14, "gate_exp:1": 15, "gates:1": 16, "gT:1": 24,
      "fin:0": 38, "stats:a": 38, "n:a": 41, "nT": 43, "qkv0": 45, "qkv1": 46, "rope": 46,
      "split": 51, "kT": 54, "qT0": 55, "qT1": 56, "qT2": 57, "qT3": 58}


class Place:

    def __init__(self, turn, hold, links=(0, 0)):
        self.turn = turn
        self.hold = hold
        self.chunk = hold(turn * (2 * FFN_CHUNKS) + FFN_CHUNKS)
        self.unit = hold(turn * (2 * EXPERTS) + EXPERTS)
        self.ffn = hold(turn * 2 + 1)
        self.added = hold(turn * (2 * (EXPERTS - 1)) + (EXPERTS - 1))
        self.att = hold(turn * 1)
        self.groups = hold(turn * GROUPS)
        self.tiles = hold(turn * (GROUPS * TILES))
        self.scores = hold(turn * (2 * GROUPS * TILES))
        self.maxes = hold(turn * (GROUPS * NMAX))
        self.misc = hold(turn * len(MISC_TURN) + len(MISC_FIRST))
        self.next_att = hold(turn * 1 + 1)
        self.stats = hold(turn * 3 + 2)
        self.nth = {"0": 0, "1": 1, "a": 2}
        self.links = hold(turn * links[1] + links[0])
        self.first_kind = 0
        self.names = MISC_TURN


class First(Place):

    def __init__(self):
        self.turn = -1
        self.chunk = self.unit = self.ffn = self.added = self.att = self.groups = 0
        self.tiles = self.scores = self.maxes = self.misc = self.stats = self.links = 0
        self.first_kind = 0
        self.next_att = 0
        self.nth = {"0": 0, "a": 1}
        self.names = MISC_FIRST


class Last(Place):

    def __init__(self, links=(0, 0)):
        super().__init__(TURNS, lambda value: value, links)
        self.first_kind = 1
        self.nth = {"1": 0}
        self.names = MISC_LAST


POOL_LINKS = (12, 14)
DVE_LINKS = (50, 110)


CONST_LOADS = 15


def counted(found, stated, name):
    assert found == stated, f"{name}: {found}, not {stated}"


def build(nc, x, wq, wk, wv, wo, gamma, beta, Wg, W1, b1, W2, b2,
          ident_d, mask_d, maskT_d, rope_d, rank_d, pick_d, out):
    with ExitStack() as ctx:
        def sb(name, shape, dt=F32):
            return ctx.enter_context(nc.sbuf_tensor(name, shape, dt))

        def sem(name):
            return ctx.enter_context(nc.semaphore(name))

        psum = ctx.enter_context(nc.psum_tensor("psum", [P, 8, 512], F32))

        ident = sb("ident", [P, P])
        ident16 = sb("ident16", [P, P], BF16)
        mask_f = sb("mask_f", [P, 2, P])
        mask16 = sb("mask16", [P, 2, P], BF16)
        rope = sb("rope", [P, TILES, 2, HALF])
        spare = sb("spare", [P, 1])
        rank = sb("rank", [P, EXPERTS])
        pick_f = sb("pick_f", [2 * EXPERTS, EXPERTS, P])
        pick = sb("pick", [2 * EXPERTS, EXPERTS, P], F32R)
        eps = sb("eps", [P, TILES])
        power = sb("power", [P, TILES])
        small = sb("small", [50, P])
        smallT = sb("smallT", [P, 50])
        w1_hi = sb("w1_hi", [P, EXPERTS, F], F32R)
        w1_lo = sb("w1_lo", [P, EXPERTS, F], F32R)
        w2_hi = sb("w2_hi", [P, EXPERTS, CHUNKS, D], F32R)
        w2_lo = sb("w2_lo", [P, EXPERTS, CHUNKS, D], F32R)
        wqkv = sb("wqkv", [P, QKV])
        wo_s = sb("wo_s", [P, D])
        b1T = smallT[:, 0:32]
        b2T = smallT[:, 32:40]
        WgT = smallT[:, 40:48]
        gammaT = smallT[:, 48:49]
        betaT = smallT[:, 49:50]
        x_in = sb("x_in", [P, TILES, D])
        x1 = sb("x1", [P, TILES, D])
        x2 = sb("x2", [P, TILES, D])
        x_out = sb("x_out", [P, TILES, D])
        stats = sb("stats", [P, TILES, 6])
        mv = sb("mv", [P, TILES, 2])
        vt = sb("vt", [P, 6, TILES])
        nrm = sb("nrm", [P, TILES, D])
        z = sb("z", [P, TILES, D])
        res = [sb(f"res{k}", [P, TILES, D]) for k in range(2)]
        xn = sb("xn", [P, S])
        xn_hi = [sb(f"xn_hi{k}", [P, S], F32R) for k in range(2)]
        xn_lo = [sb(f"xn_lo{k}", [P, S], F32R) for k in range(2)]
        gs = sb("gs", [P, 10, TILES, EXPERTS])
        gr = sb("gr", [P, 8, TILES])
        gaug = sb("gaug", [P, TILES, 2 * EXPERTS])
        gT = [sb(f"gT{k}", [2 * EXPERTS, S], F32R) for k in range(2)]
        h = sb("h", [P, 2, S])
        h_hi = sb("h_hi", [P, CHUNKS, S], F32R)
        h_lo = sb("h_lo", [P, CHUNKS, S], F32R)
        gate = sb("gate", [P, 2, S])
        part = sb("part", [P, 2, S])
        acc = [sb(f"acc{k}", [P, S]) for k in range(2)]
        na = sb("na", [P, TILES, D])
        nT = sb("nT", [P, S])
        qk = sb("qk", [P, TILES, QK])
        turned = sb("turned", [P, 4, TILES, ROPED, HALF])
        rot = sb("rot", [P, TILES, ROPED, HD])
        aug = sb("aug", [P, TILES, ROPED, SLOT])
        v = sb("v", [P, TILES, KV, SLOT])
        kT = sb("kT", [P, S], F32R)
        qT = sb("qT", [P, GROUPS, S], F32R)
        q2T = sb("q2T", [P, 2, S], F32R)
        negmax = sb("negmax", [P, TILES, HEADS])
        negmax4 = sb("negmax4", [P, KV, 4])
        probs = sb("probs", [P, 2, KV, S])
        arrived = probs[:].rearrange("p a h s -> p (a h) s")

        def w1_f(e):
            return arrived[:, 2 * (e % 4)]

        def w2_f(e):
            return arrived[:, 2 * (e % 4) + 1]

        u = sb("u", [P, S])
        rden = sb("rden", [P, TILES, KV])
        ao = sb("ao", [P, TILES, D])
        aoT = sb("aoT", [P, S])

        const_loaded = sem("const_loaded")
        expert_loaded = [sem(f"expert_loaded{e}") for e in range(EXPERTS)]
        x_loaded = sem("x_loaded")
        x_out_free = sem("x_out_free")
        ones_set = sem("ones_set")
        consts_cast = sem("consts_cast")
        small_turned = sem("small_turned")
        small_ready = sem("small_ready")
        w_hi_ready = sem("w_hi_ready")
        w_lo_ready = sem("w_lo_ready")
        dve_link = sem("dve_link")
        pool_link = sem("pool_link")
        stats_ready = sem("stats_ready")
        scale_ready = sem("scale_ready")
        z_ready = sem("z_ready")
        res_ready = sem("res_ready")
        xn_ready = sem("xn_ready")
        gates_ready = sem("gates_ready")
        n_ready = sem("n_ready")
        rotated = sem("rotated")
        aug_ready = sem("aug_ready")
        misc_full = sem("misc_full")
        misc_taken = sem("misc_taken")
        gate_exp = sem("gate_exp")
        up_done = sem("up_done")
        down_done = sem("down_done")
        gate_spread = sem("gate_spread")
        gate_copied = sem("gate_copied")
        gelu_done = sem("gelu_done")
        split_done = sem("split_done")
        scaled = sem("scaled")
        added = sem("added")
        max_full = sem("max_full")
        max_taken = sem("max_taken")
        max_split = sem("max_split")
        scores_full = sem("scores_full")
        exp_done = sem("exp_done")
        pv_done = sem("pv_done")
        u_copied = sem("u_copied")

        block = ctx.enter_context(nc.Block())

        def misc(n=512):
            return psum[:, MISC_BANK, 0:n]

        def misc_at(p, name):
            return p.misc + p.names.index(name)

        def wait(eng, s, value):
            if not isinstance(value, int) or value > 0:
                eng.wait_ge(s, value)

        def hooks(steps, m, p):
            for name, step in steps.items():
                if AT[name] == m:
                    step(p)

        def heads_of(t, g):
            return t[:, :, g * KV:(g + 1) * KV, :]

        @block.sync
        def _(sp):
            def load(seq):
                sp.dma_start(x_in[:], x[seq].rearrange("(i p) d -> p i d", p=P)).then_inc(x_loaded, 16)

            def store(seq):
                sp.dma_start(out[seq].rearrange("(i p) d -> p i d", p=P), x_out[:]).then_inc(x_out_free, 16)

            load(0)
            for dst, src in ((small[0:32], b1.rearrange("e (c p) -> (e c) p", p=P)), (small[32:40], b2),
                             (small[40:48], Wg), (small[48:49], gamma[None, :]),
                             (small[49:50], beta[None, :]), (rank[:], rank_d), (pick_f[:], pick_d)):
                sp.dma_start(dst, src).then_inc(const_loaded, 16)
            for e in range(EXPERTS):
                if e >= 4:
                    sp.wait_ge(w_lo_ready, e - 3)
                sp.dma_start(w1_f(e), W1[e]).then_inc(expert_loaded[e], 16)
                sp.dma_start(w2_f(e).rearrange("p (c d) -> p c d", c=CHUNKS),
                             W2[e].rearrange("(c p) d -> p c d", p=P)).then_inc(expert_loaded[e], 16)
            sp.wait_ge(res_ready, 1)
            load(1)
            with sp.Fori(0, TURNS - 1) as turn:
                p = Place(turn, sp.snap)
                sp.wait_ge(res_ready, p.ffn + 1)
                load(turn + 2)
                sp.wait_ge(misc_taken, misc_at(p, "fin:1") + 1)
                store(turn)
            p = Place(TURNS - 1, int)
            sp.wait_ge(misc_taken, misc_at(p, "fin:1") + 1)
            store(TURNS - 1)
            p = Last()
            sp.wait_ge(misc_taken, misc_at(p, "fin:1") + 1)
            store(TURNS)
            sp.wait_ge(x_out_free, 16 + 16 * SEQS)

        @block.gpsimd
        def _(pool):
            at = [0]
            base = [0]

            def link(ins):
                at[0] += 1
                ins.then_inc(pool_link, 1)
                pool.wait_ge(pool_link, base[0] + at[0])

            for ins in (pool.memset(eps[:], EPS), pool.memset(power[:], -0.5), pool.memset(aug[:], 0.0),
                        pool.memset(v[:], 0.0)):
                link(ins)
            pool.memset(x_out[:], 0.0).then_inc(x_out_free, 16)
            pool.memset(aug[:, :, HEADS:ROPED, STACK:STACK + 2], 1.0)
            pool.memset(v[:, :, :, HD:HD + 1], 1.0).then_inc(ones_set, 1)

            def norm_scale(p, nth):
                wait(pool, stats_ready, p.stats + p.nth[nth] + 1)
                t = [vt[:, k] for k in range(6)]
                link(pool.tensor_tensor(t[0], mv[:, :, 1], eps[:], ALU.add))
                r = pool.tensor_tensor(t[1], t[0], power[:], ALU.pow)
                if nth != "a":
                    link(r)
                    link(pool.tensor_tensor(t[2], t[1], t[1], ALU.mult))
                    link(pool.tensor_tensor(t[3], t[2], mv[:, :, 1], ALU.mult))
                    link(pool.tensor_tensor(t[4], t[3], eps[:], ALU.add))
                    link(pool.tensor_tensor(t[2], t[4], power[:], ALU.pow))
                    r = pool.tensor_tensor(t[5], t[2], t[1], ALU.mult)
                r.then_inc(scale_ready, 1)

            def rotate(p):
                wait(pool, misc_taken, misc_at(p, "qkv1") + 1)
                t = qk[:].rearrange("p i (h a c) -> p i h a c", a=2, c=HALF)
                for n, (a, b) in enumerate(((0, 0), (1, 1), (0, 1), (1, 0))):
                    for i in range(TILES):
                        cs = rope[:, i, b, None, :].broadcast_to([P, ROPED, HALF])
                        ins = pool.tensor_tensor(turned[:, n, i], t[:, i, :, a, :], cs, ALU.mult)
                link(ins)
                for i in range(TILES):
                    pool.tensor_tensor(rot[:, i, :, 0:HALF], turned[:, 0, i], turned[:, 1, i], ALU.subtract)
                for i in range(TILES):
                    ins = pool.tensor_tensor(rot[:, i, :, HALF:HD], turned[:, 2, i], turned[:, 3, i], ALU.add)
                ins.then_inc(rotated, 1)

            def add(p, n):
                k, e = n // EXPERTS, n % EXPERTS
                if e == 0:
                    return
                sums = p.added + (EXPERTS - 1) * k
                total = acc[k + p.first_kind]
                wait(pool, scaled, p.unit + n + 1)
                if e == 1:
                    pool.tensor_tensor(total[:], part[:, 0], part[:, 1], ALU.add).then_inc(added, 1)
                else:
                    wait(pool, added, sums + (e - 1))
                    pool.tensor_tensor(total[:], total[:], part[:, e % 2], ALU.add).then_inc(added, 1)

            def ffns(p, count, steps):
                for m in range(count * FFN_CHUNKS):
                    if m >= LAG and (m - LAG) % CHUNKS == CHUNKS - 1:
                        add(p, (m - LAG) // CHUNKS)
                    hooks(steps, m, p)
                add(p, count * EXPERTS - 1)

            p = First()
            norm_scale(p, "0")
            ffns(p, 1, {})
            norm_scale(p, "a")
            rotate(p)
            counted(at[0], POOL_LINKS[0], "POOL_LINKS, first")
            with pool.Fori(0, TURNS) as turn:
                p = Place(turn, pool.snap, POOL_LINKS)
                at[0], base[0] = 0, p.links
                norm_scale(p, "0")
                ffns(p, 2, {"stats:1": lambda p: norm_scale(p, "1"),
                            "stats:a": lambda p: norm_scale(p, "a"), "rope": rotate})
                counted(at[0], POOL_LINKS[1], "POOL_LINKS")
            p = Last(POOL_LINKS)
            at[0], base[0] = 0, p.links
            norm_scale(p, "1")
            ffns(p, 1, {})

        @block.scalar
        def _(act):
            for dst, src in ((ident[:], ident_d), (mask_f[:, 0], mask_d), (mask_f[:, 1], maskT_d),
                             (rope[:], rope_d), (wqkv[:, 0:D], wq), (wqkv[:, D:D + KV * HD], wk),
                             (wqkv[:, QK:QKV], wv), (wo_s[:], wo)):
                act.dma_start(dst, src).then_inc(const_loaded, 16)
            act.wait_ge(small_turned, 1)
            act.activation(smallT[:], misc(50), ACT.Copy).then_inc(small_ready, 1)
            act.wait_ge(small_ready, 1)
            act.wait_ge(ones_set, 1)

            def weights_hi(e):
                act.wait_ge(expert_loaded[e], 32)
                act.activation(w1_hi[:, e], w1_f(e), ACT.Copy)
                act.activation(w2_hi[:, e].rearrange("p c d -> p (c d)"), w2_f(e), ACT.Copy).then_inc(w_hi_ready, 1)

            def take(p, name, *pairs):
                wait(act, misc_full, misc_at(p, name) + 1)
                for dst, src in pairs:
                    ins = act.activation(dst, src, ACT.Copy)
                ins.then_inc(misc_taken, 1)

            def take_z(p, k):
                wait(act, misc_full, misc_at(p, f"zT:{k}") + 1)
                wait(act, xn_ready, p.ffn + (k - p.first_kind))
                act.activation(xn[:], misc(), ACT.Identity, bias=betaT, scale=gammaT)
                act.activation(xn_hi[k][:], misc(), ACT.Identity, bias=betaT, scale=gammaT)\
                   .then_inc(misc_taken, 1)

            def exp_gate(p, k):
                wait(act, misc_taken, misc_at(p, f"logits:{k}") + 1)
                act.activation(gs[:, 1], gs[:, 0], ACT.Exp).then_inc(gate_exp, 1)

            def take_gates(p, k):
                take(p, f"gT:{k}", (gT[k][:], psum[0:2 * EXPERTS, MISC_BANK, :]))

            def take_qkv(p, half):
                src = misc(2 * QKV).rearrange("p (i c) -> p i c", i=2)
                t = slice(2 * half, 2 * half + 2)
                wait(act, misc_full, misc_at(p, f"qkv{half}") + 1)
                for i in range(2):
                    act.activation(v[:, 2 * half + i, :, 0:HD],
                                   src[:, i, QK:QKV].rearrange("p (h d) -> p h d", h=KV), ACT.Copy)
                act.activation(qk[:, t], src[:, :, 0:QK], ACT.Copy).then_inc(misc_taken, 1)

            def gelu(p, m):
                e, c = m // CHUNKS % EXPERTS, m % CHUNKS
                wait(act, up_done, p.chunk + m + 1)
                wait(act, split_done, p.chunk + (m - 1))
                bias = b1T[:, CHUNKS * e + c:CHUNKS * e + c + 1]
                if c == CHUNKS - 1:
                    wait(act, down_done, p.chunk + (m - CHUNKS + 1))
                    act.activation(h_hi[:, c], psum[:, UP_BANK + m % 2], ACT.Gelu_apprx_tanh, bias=bias)
                act.activation(h[:, m % 2], psum[:, UP_BANK + m % 2], ACT.Gelu_apprx_tanh, bias=bias)\
                   .then_inc(gelu_done, 1)

            def copy_gate(p, n):
                wait(act, gate_spread, p.unit + n + 1)
                wait(act, scaled, p.unit + (n - 1))
                act.activation(gate[:, n % 2], psum[:, GATE_BANK], ACT.Copy).then_inc(gate_copied, 1)

            def ffns(p, count, steps, first=False):
                for m in range(count * FFN_CHUNKS):
                    if first and m % CHUNKS == 0 and m // CHUNKS + 2 < EXPERTS:
                        weights_hi(m // CHUNKS + 2)
                    gelu(p, m)
                    if m % CHUNKS == 0:
                        copy_gate(p, m // CHUNKS)
                    hooks(steps, m, p)

            def copy_u(p, g):
                wait(act, pv_done, p.tiles + TILES * (g + 1))
                if g > 0:
                    wait(act, misc_full, misc_at(p, f"uT{g - 1}") + 1)
                act.activation(u[:], psum[:, PV_BANK], ACT.Copy).then_inc(u_copied, 1)

            def take_q2(p, g):
                take(p, f"q2T{g}", (q2T[:, g % 2], misc()))

            def take_o(p):
                take(p, "aT", (aoT[:], misc()))

            def attend(p, prepares):
                take_q2(p, 0)
                for g in range(GROUPS):
                    for j in range(TILES):
                        for pair in range(2):
                            s, n = 2 * (TILES * g + j) + pair, S - P * j
                            wait(act, scores_full, p.scores + s + 1)
                            if TILES * g + j >= 2:
                                wait(act, pv_done, p.tiles + (TILES * g + j - 1))
                            b = SCORE_BANK + 2 * pair
                            act.activation(probs[:, j % 2, 2 * pair:2 * pair + 2, 0:n],
                                           psum[:, b:b + 2, 0:n], ACT.Exp, scale=SCALE)\
                               .then_inc(exp_done, 1)
                        if j == 0 and g > 0:
                            copy_u(p, g - 1)
                        if j == 0 and g == 1 and prepares:
                            take_z(p, 0)
                        if j == 1 and g < GROUPS - 1:
                            take_q2(p, g + 1)
                        if j == 2 and g == 2 and prepares:
                            exp_gate(p, 0)
                    if g == GROUPS - 1 and prepares:
                        take_gates(p, 0)

            after = {"nT": lambda p: take(p, "nT", (nT[:], misc())),
                     "qkv0": lambda p: take_qkv(p, 0), "qkv1": lambda p: take_qkv(p, 1),
                     "kT": lambda p: take(p, "kT", (kT[:], misc()))}
            for g in range(GROUPS):
                after[f"qT{g}"] = lambda p, g=g: take(p, f"qT{g}", (qT[:, g], misc()))
            between = {"copy_u3": lambda p: copy_u(p, GROUPS - 1), "aT": take_o,
                       "zT:1": lambda p: take_z(p, 1), "gate_exp:1": lambda p: exp_gate(p, 1),
                       "gT:1": lambda p: take_gates(p, 1)}

            p = First()
            weights_hi(0)
            weights_hi(1)
            take_z(p, 0)
            exp_gate(p, 0)
            take_gates(p, 0)
            ffns(p, 1, {}, first=True)
            for step in after.values():
                step(p)
            with act.Fori(0, TURNS) as turn:
                p = Place(turn, act.snap)
                attend(p, True)
                ffns(p, 2, between | after)
            p = Last()
            attend(p, False)
            for step in between.values():
                step(p)
            ffns(p, 1, {})

        @block.vector
        def _(dve):
            at = [0]
            base = [0]

            def link(ins):
                at[0] += 1
                ins.then_inc(dve_link, 1)
                dve.wait_ge(dve_link, base[0] + at[0])

            def along(col, n):
                return col[:, :, None].broadcast_to([P, TILES, n])

            def weights_lo(e):
                dve.wait_ge(w_hi_ready, e + 1)
                dve.tensor_tensor(w1_lo[:, e], w1_f(e), w1_hi[:, e].bitcast(F32), ALU.subtract)
                dve.tensor_tensor(w2_lo[:, e].rearrange("p c d -> p (c d)"), w2_f(e),
                                  w2_hi[:, e].rearrange("p c d -> p (c d)").bitcast(F32), ALU.subtract)\
                   .then_inc(w_lo_ready, 1)

            def statistics(src):
                for i in range(TILES):
                    ins = dve.bn_stats(stats[:, i], src[:, i])
                link(ins)
                dve.memset(spare[:], 0.0)
                for i in range(TILES):
                    ins = dve.bn_aggr(mv[:, i], stats[:, i])
                ins.then_inc(stats_ready, 1)

            def normalize(dst, src, scale):
                for i in range(TILES):
                    ins = dve.tensor_scalar(dst[:, i], src[:, i], mv[:, i, 0:1], scale[:, i:i + 1],
                                            ALU.subtract, ALU.mult)
                return ins

            def make_z(p, k, src):
                wait(dve, scale_ready, p.stats + p.nth[str(k)] + 1)
                link(normalize(nrm, src, vt[:, 1]))
                normalize(z, src, vt[:, 5]).then_inc(z_ready, 1)
                dve.scalar_tensor_tensor(res[k][:], nrm[:], 0.5, src[:], ALU.mult, ALU.add)\
                   .then_inc(res_ready, 1)

            def make_xlo(p, k):
                wait(dve, misc_taken, misc_at(p, f"zT:{k}") + 1)
                dve.tensor_tensor(xn_lo[k][:], xn[:], xn_hi[k][:].bitcast(F32), ALU.subtract)\
                   .then_inc(xn_ready, 1)

            def shift_logits(p, k):
                wait(dve, misc_full, misc_at(p, f"logits:{k}") + 1)
                logits = misc(TILES * EXPERTS).rearrange("p (i e) -> p i e", i=TILES)
                link(dve.tensor_reduce(gr[:, 0], logits, AX_X, ALU.max))
                dve.tensor_tensor(gs[:, 0], logits, along(gr[:, 0], EXPERTS), ALU.subtract)\
                   .then_inc(misc_taken, 1)

            def make_gates(p, k):
                wait(dve, gate_exp, p.ffn + (k - p.first_kind) + 1)
                first = [gs[:, n] for n in range(10)]
                _, ex, pr, eq, one1, left, one2, both, share, _ = first
                ranks = rank[:, None, :].broadcast_to([P, TILES, EXPERTS])
                link(dve.tensor_reduce(gr[:, 1], ex, AX_X, ALU.add))
                link(dve.reciprocal(gr[:, 2], gr[:, 1]))
                link(dve.tensor_tensor(pr, ex, along(gr[:, 2], EXPERTS), ALU.mult))

                def pick_largest(values, top, one):
                    link(dve.tensor_reduce(top, values, AX_X, ALU.max))
                    link(dve.tensor_tensor(eq, values, along(top, EXPERTS), ALU.is_equal))
                    link(dve.tensor_tensor(both, eq, ranks, ALU.mult))
                    link(dve.tensor_reduce(gr[:, 5], both, AX_X, ALU.max))
                    link(dve.tensor_tensor(one, ranks, along(gr[:, 5], EXPERTS), ALU.is_equal))

                pick_largest(pr, gr[:, 3], one1)
                link(dve.scalar_tensor_tensor(left, one1, -2.0, pr, ALU.mult, ALU.add))
                pick_largest(left, gr[:, 4], one2)
                link(dve.tensor_tensor(gr[:, 6], gr[:, 3], gr[:, 4], ALU.add))
                link(dve.tensor_scalar(gr[:, 6], gr[:, 6], GATE_EPS, None, ALU.add))
                link(dve.reciprocal(gr[:, 7], gr[:, 6]))
                link(dve.tensor_tensor(both, one1, one2, ALU.add))
                link(dve.tensor_tensor(both, both, pr, ALU.mult))
                link(dve.tensor_tensor(share, both, along(gr[:, 7], EXPERTS), ALU.mult))
                hi = gaug[:, :, 0:EXPERTS]
                link(dve.tensor_copy(hi.bitcast(F32R), share))
                dve.tensor_tensor(gaug[:, :, EXPERTS:2 * EXPERTS], share, hi, ALU.subtract)\
                   .then_inc(gates_ready, 1)

            def split(p, m):
                c = m % CHUNKS
                wait(dve, gelu_done, p.chunk + m + 1)
                wait(dve, down_done, p.chunk + (m - CHUNKS + 1))
                if c < CHUNKS - 1:
                    link(dve.tensor_copy(h_hi[:, c], h[:, m % 2]))
                dve.tensor_tensor(h_lo[:, c], h[:, m % 2], h_hi[:, c].bitcast(F32), ALU.subtract)\
                   .then_inc(split_done, 1)

            def scale(p, n):
                e = n % EXPERTS
                sums = p.added + (EXPERTS - 1) * (n // EXPERTS)
                wait(dve, down_done, p.chunk + CHUNKS * (n + 1))
                wait(dve, gate_copied, p.unit + n + 1)
                wait(dve, added, sums + (max(e - 2, 1) if e > 1 else 0))
                dve.scalar_tensor_tensor(part[:, e % 2], psum[:, Y_BANK + n % 2], b2T[:, e:e + 1],
                                         gate[:, n % 2], ALU.add, ALU.mult).then_inc(scaled, 1)

            def ffns(p, count, steps, first=False):
                for m in range(count * FFN_CHUNKS):
                    if first and m % CHUNKS == 0 and m // CHUNKS + 2 < EXPERTS:
                        weights_lo(m // CHUNKS + 2)
                    split(p, m)
                    if m >= LAG and (m - LAG) % CHUNKS == CHUNKS - 1:
                        scale(p, (m - LAG) // CHUNKS)
                    hooks(steps, m, p)
                scale(p, count * EXPERTS - 1)

            def finish(p, k, dst):
                wait(dve, misc_full, misc_at(p, f"fin:{k}") + 1)
                if k == 1:
                    wait(dve, x_out_free, p.turn * 16 + 16)
                ins = dve.scalar_tensor_tensor(dst[:].rearrange("p i d -> p (i d)"), misc(), 0.5,
                                               res[k][:].rearrange("p i d -> p (i d)"), ALU.mult, ALU.add)
                ins.then_inc(misc_taken, 1)
                dve.wait_ge(misc_taken, misc_at(p, f"fin:{k}") + 1)

            def norm_for_attention(p):
                wait(dve, scale_ready, p.stats + p.nth["a"] + 1)
                normalize(na, x1, vt[:, 1]).then_inc(n_ready, 1)

            def stack(p):
                wait(dve, rotated, p.next_att + 1)
                for h0, h1, his, lo in ((0, HEADS, (0, HD), 2 * HD), (HEADS, ROPED, (0, 2 * HD), HD)):
                    for a in his:
                        ins = dve.tensor_copy(aug[:, :, h0:h1, a:a + HD].bitcast(F32R), rot[:, :, h0:h1])
                link(ins)
                for h0, h1, his, lo in ((0, HEADS, (0, HD), 2 * HD), (HEADS, ROPED, (0, 2 * HD), HD)):
                    ins = dve.tensor_tensor(aug[:, :, h0:h1, lo:lo + HD], rot[:, :, h0:h1],
                                            aug[:, :, h0:h1, 0:HD], ALU.subtract)
                ins.then_inc(aug_ready, 1)

            def take_max(p, g, k):
                kv, tiles = MAX_BLOCKS[k]
                x_at, head = NMAX * g + k, g * KV + kv
                wait(dve, max_full, p.maxes + x_at + 1)
                bank = psum[:, MAX_BANK + x_at % 2]
                if len(tiles) > 1:
                    ins = dve.tensor_reduce(negmax4[:, kv], bank.rearrange("p (k n) -> p k n", n=P),
                                            AX_X, ALU.max, negate=True)
                else:
                    tile = tiles[0][0]
                    ins = dve.tensor_reduce(negmax[:, tile, head:head + 1], bank[:, 0:P * (tile + 1)],
                                            AX_X, ALU.max, negate=True)
                ins.then_inc(max_taken, 1)

            def split_max(p, g):
                dve.wait_ge(max_taken, p.maxes + NMAX * (g + 1))
                heads = slice(g * KV, (g + 1) * KV)
                dve.tensor_copy(negmax[:, 0, heads], negmax4[:, :, 0])
                link(dve.tensor_reduce(negmax[:, 2, heads], negmax4[:, :, 1:4], AX_X, ALU.min))
                src = negmax[:, :, heads, None]
                hi = heads_of(aug, g)[:, :, :, STACK:STACK + 1]
                link(dve.tensor_copy(hi.bitcast(F32R), src))
                dve.tensor_tensor(heads_of(aug, g)[:, :, :, STACK + 1:STACK + 2], src, hi, ALU.subtract)\
                   .then_inc(max_split, 1)

            def divide(p, g):
                wait(dve, misc_full, misc_at(p, f"uT{g}") + 1)
                src = misc().rearrange("p (i h c) -> p i h c", i=TILES, h=KV)
                link(dve.reciprocal(rden[:], src[:, :, :, HD]))
                dst = ao[:].rearrange("p i (g h d) -> p i g h d", g=GROUPS, h=KV)[:, :, g]
                dve.tensor_tensor(dst, src[:, :, :, 0:HD],
                                  rden[:, :, :, None].broadcast_to([P, TILES, KV, HD]), ALU.mult)\
                   .then_inc(misc_taken, 1)

            def attend(p, prepares):
                for g in range(2):
                    for k in range(NMAX):
                        take_max(p, g, k)
                    split_max(p, g)
                if prepares:
                    dve.wait_ge(x_loaded, (p.turn + 2) * 16)
                    statistics(x_in)
                for g in range(GROUPS):
                    if g + 2 < GROUPS:
                        for k in range(NMAX):
                            take_max(p, g + 2, k)
                        split_max(p, g + 2)
                    if g == 0 and prepares:
                        make_z(p, 0, x_in)
                    if g == 1 and prepares:
                        make_xlo(p, 0)
                    if g > 0:
                        divide(p, g - 1)
                    if g == 1 and prepares:
                        shift_logits(p, 0)
                    if g == 2 and prepares:
                        make_gates(p, 0)

            def add_attention(p):
                wait(dve, misc_full, misc_at(p, "y") + 1)
                dve.tensor_tensor(x2[:].rearrange("p i d -> p (i d)"), misc(),
                                  x1[:].rearrange("p i d -> p (i d)"), ALU.add).then_inc(misc_taken, 1)
                dve.wait_ge(misc_taken, misc_at(p, "y") + 1)

            between = {"norm3": lambda p: divide(p, GROUPS - 1), "y": add_attention,
                       "stats:1": lambda p: statistics(x2), "z:1": lambda p: make_z(p, 1, x2),
                       "xlo:1": lambda p: make_xlo(p, 1), "logits:1": lambda p: shift_logits(p, 1),
                       "gates:1": lambda p: make_gates(p, 1)}
            after = {"fin:0": lambda p: finish(p, 0, x1), "stats:a": lambda p: statistics(x1),
                     "n:a": norm_for_attention, "split": stack}

            dve.wait_ge(const_loaded, 16 * CONST_LOADS)
            dve.tensor_copy(ident16[:], ident[:])
            dve.tensor_copy(mask16[:], mask_f[:])
            dve.tensor_copy(pick[:], pick_f[:]).then_inc(consts_cast, 1)
            p = First()
            dve.wait_ge(x_loaded, 16)
            statistics(x_in)
            make_z(p, 0, x_in)
            dve.wait_ge(small_ready, 1)
            make_xlo(p, 0)
            shift_logits(p, 0)
            make_gates(p, 0)
            weights_lo(0)
            weights_lo(1)
            ffns(p, 1, {}, first=True)
            for step in after.values():
                step(p)
            counted(at[0], DVE_LINKS[0], "DVE_LINKS, first")
            with dve.Fori(0, TURNS) as turn:
                p = Place(turn, dve.snap, DVE_LINKS)
                at[0], base[0] = 0, p.links
                attend(p, True)
                ffns(p, 2, between | after)
                finish(p, 1, x_out)
                counted(at[0], DVE_LINKS[1], "DVE_LINKS, turn")
            p = Last(DVE_LINKS)
            at[0], base[0] = 0, p.links
            attend(p, False)
            for step in between.values():
                step(p)
            ffns(p, 1, {})
            finish(p, 1, x_out)

        @block.tensor
        def _(pe):
            mm = nc.tensor.matmul

            def use_misc(p, name):
                wait(pe, misc_taken, misc_at(p, name))

            def turn_tiles(p, name, parts, rows=P):
                use_misc(p, name)
                for i, part_i in enumerate(parts):
                    ins = nc.tensor.transpose(psum[0:rows, MISC_BANK, i * P:(i + 1) * P], part_i, ident[:])
                ins.then_inc(misc_full, 1)

            def turn_z(p, k):
                wait(pe, z_ready, p.ffn + (k - p.first_kind) + 1)
                turn_tiles(p, f"zT:{k}", [z[:, i] for i in range(TILES)])

            def make_logits(p, k):
                use_misc(p, f"logits:{k}")
                for i in range(TILES):
                    ins = mm(psum[:, MISC_BANK, i * EXPERTS:(i + 1) * EXPERTS], xn[:, i * P:(i + 1) * P],
                             WgT, start=True, stop=True)
                ins.then_inc(misc_full, 1)

            def turn_gates(p, k):
                wait(pe, gates_ready, p.ffn + (k - p.first_kind) + 1)
                turn_tiles(p, f"gT:{k}", [gaug[:, i] for i in range(TILES)], 2 * EXPERTS)

            def up(p, m, first):
                n, e, c = m // CHUNKS, m // CHUNKS % EXPERTS, m % CHUNKS
                k = n // EXPERTS + p.first_kind
                if m % FFN_CHUNKS == 0:
                    wait(pe, xn_ready, p.ffn + (k - p.first_kind) + 1)
                    wait(pe, misc_taken, misc_at(p, f"gT:{k}") + 1)
                if first and c == 0:
                    pe.wait_ge(w_lo_ready, e + 1)
                if c == 0:
                    wait(pe, gate_copied, p.unit + n)
                    mm(psum[:, GATE_BANK], pick[:, e], gT[k][:], start=True, stop=True)\
                        .then_inc(gate_spread, 1)
                wait(pe, gelu_done, p.chunk + (m - 1))
                o, cols = psum[:, UP_BANK + m % 2], slice(c * P, (c + 1) * P)
                mm(o, w1_hi[:, e, cols], xn_hi[k][:], start=True, stop=False)
                mm(o, w1_hi[:, e, cols], xn_lo[k][:], start=False, stop=False)
                mm(o, w1_lo[:, e, cols], xn_hi[k][:], start=False, stop=True).then_inc(up_done, 1)

            def down(p, m):
                n, e, c = m // CHUNKS, m // CHUNKS % EXPERTS, m % CHUNKS
                wait(pe, split_done, p.chunk + m + 1)
                if c == 0:
                    wait(pe, scaled, p.unit + (n - 1))
                o = psum[:, Y_BANK + n % 2]
                mm(o, w2_hi[:, e, c], h_hi[:, c], start=(c == 0), stop=False)
                mm(o, w2_hi[:, e, c], h_lo[:, c], start=False, stop=False)
                mm(o, w2_lo[:, e, c], h_hi[:, c], start=False, stop=(c == CHUNKS - 1)).then_inc(down_done, 1)

            def ffns(p, count, steps, first=False):
                for m in range(count * FFN_CHUNKS):
                    up(p, m, first)
                    if m >= LAG:
                        down(p, m - LAG)
                    hooks(steps, m, p)
                for m in range(count * FFN_CHUNKS - LAG, count * FFN_CHUNKS):
                    down(p, m)

            def finish(p, k):
                wait(pe, added, p.added + (EXPERTS - 1) * (k - p.first_kind + 1))
                turn_tiles(p, f"fin:{k}", [acc[k][:, i * P:(i + 1) * P] for i in range(TILES)])

            def turn_n(p):
                wait(pe, n_ready, p.next_att + 1)
                turn_tiles(p, "nT", [na[:, i] for i in range(TILES)])

            def project(p, half):
                use_misc(p, f"qkv{half}")
                for i in range(2):
                    t = 2 * half + i
                    ins = mm(psum[:, MISC_BANK, i * QKV:(i + 1) * QKV], nT[:, t * P:(t + 1) * P], wqkv[:],
                             start=True, stop=True)
                ins.then_inc(misc_full, 1)

            def turn_heads(p, name, h0):
                turn_tiles(p, name, [aug[:, i, h0:h0 + KV].rearrange("p h c -> p (h c)")
                                     for i in range(TILES)])

            def turn_keys(p):
                wait(pe, aug_ready, p.next_att + 1)
                turn_heads(p, "kT", HEADS)

            def block_max(p, g, k):
                kv, tiles = MAX_BLOCKS[k]
                x_at = NMAX * g + k
                if x_at >= 2:
                    wait(pe, max_taken, p.maxes + (x_at - 1))
                bank = MAX_BANK + x_at % 2
                rows = slice(SLOT * kv, SLOT * kv + STACK)
                for tile, col in tiles:
                    n = P * (tile + 1)
                    mm(psum[:, bank, col:col + n], qT[rows, g, tile * P:(tile + 1) * P], kT[rows, 0:n],
                       start=True, stop=False)
                    ins = mm(psum[:, bank, col + tile * P:col + n], ident16[:], mask16[:, 0],
                             start=False, stop=True)
                ins.then_inc(max_full, 1)

            def turn_q2(p, g):
                wait(pe, max_split, p.groups + g + 1)
                turn_heads(p, f"q2T{g}", g * KV)

            def score(p, g, j, pair):
                s, n = 2 * (TILES * g + j) + pair, S - P * j
                if s >= 2:
                    wait(pe, exp_done, p.scores + (s - 1))
                if s % (2 * TILES) == 0:
                    wait(pe, misc_taken, misc_at(p, f"q2T{g}") + 1)
                for i in range(2):
                    kv = 2 * pair + i
                    rows = slice(SLOT * kv, SLOT * kv + STACK + 2)
                    bank = SCORE_BANK + 2 * pair + i
                    mm(psum[:, bank, 0:n], kT[rows, j * P:(j + 1) * P], q2T[rows, g % 2, j * P:S],
                       start=True, stop=False)
                    ins = mm(psum[:, bank, 0:P], ident16[:], mask16[:, 1], start=False, stop=True)
                ins.then_inc(scores_full, 1)

            def weigh(p, g, j):
                wait(pe, exp_done, p.scores + 2 * (TILES * g + j + 1))
                if j == 0 and g > 0:
                    wait(pe, u_copied, p.groups + g)
                for kv in range(KV):
                    ins = mm(psum[SLOT * kv:SLOT * (kv + 1), PV_BANK, j * P:S], v[:, j, kv],
                             probs[:, j % 2, kv, 0:S - P * j], start=(j == 0), stop=(j == TILES - 1))
                ins.then_inc(pv_done, 1)

            def turn_u(p, g):
                wait(pe, u_copied, p.groups + g + 1)
                turn_tiles(p, f"uT{g}", [u[:, i * P:(i + 1) * P] for i in range(TILES)])

            def turn_o(p):
                turn_tiles(p, "aT", [ao[:, i] for i in range(TILES)])

            def project_o(p):
                use_misc(p, "y")
                for i in range(TILES):
                    ins = mm(psum[:, MISC_BANK, i * D:(i + 1) * D], aoT[:, i * P:(i + 1) * P], wo_s[:],
                             start=True, stop=True)
                ins.then_inc(misc_full, 1)

            def attend(p, prepares):
                wait(pe, misc_taken, p.misc)
                wait(pe, gate_copied, p.unit)
                for g in range(2):
                    for k in range(NMAX):
                        block_max(p, g, k)
                turn_q2(p, 0)
                wait(pe, gelu_done, p.chunk)
                wait(pe, scaled, p.unit)
                for g in range(GROUPS):
                    if g == 1 and prepares:
                        turn_z(p, 0)
                    for j in range(TILES):
                        for pair in range(2):
                            score(p, g, j, pair)
                            if g + 2 < GROUPS:
                                step = 2 * j + pair
                                for k in range(NMAX * step // 8, NMAX * (step + 1) // 8):
                                    block_max(p, g + 2, k)
                        if j > 0:
                            weigh(p, g, j - 1)
                        elif g > 0:
                            weigh(p, g - 1, TILES - 1)
                        if j == 1 and g < GROUPS - 1:
                            turn_q2(p, g + 1)
                        if j == 2 and g > 0:
                            turn_u(p, g - 1)
                    if g == 1 and prepares:
                        make_logits(p, 0)
                    if g == GROUPS - 1 and prepares:
                        turn_gates(p, 0)
                weigh(p, GROUPS - 1, TILES - 1)

            between = {"uT3": lambda p: turn_u(p, GROUPS - 1), "aT": turn_o, "y": project_o,
                       "zT:1": lambda p: turn_z(p, 1), "logits:1": lambda p: make_logits(p, 1),
                       "gT:1": lambda p: turn_gates(p, 1)}
            after = {"fin:0": lambda p: finish(p, 0), "nT": turn_n, "qkv0": lambda p: project(p, 0),
                     "qkv1": lambda p: project(p, 1), "kT": turn_keys}
            for g in range(GROUPS):
                after[f"qT{g}"] = lambda p, g=g: turn_heads(p, f"qT{g}", g * KV)

            pe.wait_ge(const_loaded, 16 * CONST_LOADS)
            nc.tensor.transpose(misc(50), small[:], ident[0:50, 0:50]).then_inc(small_turned, 1)
            pe.wait_ge(small_ready, 1)
            pe.wait_ge(consts_cast, 1)
            p = First()
            turn_z(p, 0)
            make_logits(p, 0)
            turn_gates(p, 0)
            ffns(p, 1, {}, first=True)
            for step in after.values():
                step(p)
            with pe.Fori(0, TURNS) as turn:
                p = Place(turn, pe.snap)
                attend(p, True)
                wait(pe, exp_done, p.scores + 2 * GROUPS * TILES)
                wait(pe, max_taken, p.maxes + GROUPS * NMAX)
                ffns(p, 2, between | after)
                finish(p, 1)
            p = Last()
            attend(p, False)
            for step in between.values():
                step(p)
            wait(pe, exp_done, p.scores + 2 * GROUPS * TILES)
            wait(pe, max_taken, p.maxes + GROUPS * NMAX)
            ffns(p, 1, {})
            finish(p, 1)


NAMES = ["L0_attn_x", "L0_attn_wq", "L0_attn_wk", "L0_attn_wv", "L0_attn_wo", "L0_ffn_gamma",
         "L0_ffn_beta", "L0_ffn_Wg", "L0_ffn_W1", "L0_ffn_b1", "L0_ffn_W2", "L0_ffn_b2"]


def shape_constants():
    f = np.float32
    at = np.arange(P)
    inverse = f(1.0) / f(10000.0) ** (np.arange(HALF, dtype=f) / f(HALF))
    angle = np.arange(S, dtype=f)[:, None] * inverse[None, :]
    rope = np.stack([np.cos(angle), np.sin(angle)], axis=1).astype(f)
    rope = rope.reshape(TILES, P, 2, HALF).transpose(1, 0, 2, 3)
    rank = np.broadcast_to(np.arange(EXPERTS, 0, -1).astype(f), (P, EXPERTS))
    pick = np.zeros((2 * EXPERTS, EXPERTS, P), f)
    for row in range(2 * EXPERTS):
        pick[row, row % EXPERTS] = 1.0
    return {"table_identity": np.eye(P, dtype=f),
            "table_mask": np.where(at[None, :] <= at[:, None], f(0.0), f(MASKED)),
            "table_mask_turned": np.where(at[None, :] >= at[:, None], f(0.0), f(MASKED)),
            "table_rope": rope, "table_rank": rank, "table_pick": pick}


def kernel(**inputs):
    import concourse.bacc as bacc
    from concourse.bass_utils import run_bass_kernel_spmd

    nc = bacc.Bacc("TRN2", target_bir_lowering=False, num_devices=1)
    arrays = {name: np.ascontiguousarray(inputs[name]) for name in NAMES}
    arrays.update({name: np.ascontiguousarray(a) for name, a in shape_constants().items()})
    args = [nc.dram_tensor(name, a.shape, mybir.dt.from_np(a.dtype), kind="ExternalInput").ap()
            for name, a in arrays.items()]
    out = nc.dram_tensor("out", (SEQS, S, D), F32, kind="ExternalOutput").ap()
    build(nc, *args, out)
    return run_bass_kernel_spmd(nc, [arrays], core_ids=[0]).results[0]["out"]
```

```python
from contextlib import ExitStack

import numpy as np

import concourse.bass as bass
from concourse import mybir

F32 = mybir.dt.float32
F32R = mybir.dt.float32r
BF16 = mybir.dt.bfloat16
ALU = mybir.AluOpType
ACT = mybir.ActivationFunctionType
AX_X = mybir.AxisListType.X

P = 128
SEQS, S, D = 8, 512, 128
TILES = S // P
EXPERTS, F = 8, 512
CHUNKS = F // P
HEADS, KV, HD = 16, 4, 8
GROUPS = HEADS // KV
HALF = HD // 2
ROPED = HEADS + KV
SLOT = P // KV
QK = ROPED * HD
QKV = QK + KV * HD
STACK = 3 * HD
EPS = 1e-5
GATE_EPS = 1e-9
MASKED = -1e30
SCALE = float(1.0 / np.sqrt(np.float32(HD)))

FFN_CHUNKS = EXPERTS * CHUNKS
LAG = 3
TURNS = SEQS - 1

UP_BANK, Y_BANK, GATE_BANK, MISC_BANK = 0, 2, 4, 7
SCORE_BANK, PV_BANK, MAX_BANK = 0, 4, 5

MAX_BLOCKS = [(0, (0, 1, 2, 3)), (1, (0, 1)), (1, (2, 3))] + \
             [(tile, (kv,)) for tile in (2, 3) for kv in range(KV)]
NMAX = len(MAX_BLOCKS)

FFN_PREP = ["zT", "logits", "gT"]
ATT_PREP = ["nT", "qkv0", "qkv1", "kT", "qT0", "qT1", "qT2", "qT3"]
ATTEND = ["q2T0", "q2T1", "zT:0", "uT0", "q2T2", "logits:0", "uT1", "q2T3", "uT2", "gT:0"]
ATTEND_END = ["uT3", "aT", "y"]
MISC_FIRST = ["zT:0", "logits:0", "gT:0", "fin:0"] + ATT_PREP
MISC_TURN = ATTEND + ATTEND_END + ["zT:1", "logits:1", "gT:1", "fin:0"] + ATT_PREP + ["fin:1"]
MISC_LAST = [x for x in ATTEND if ":" not in x] + ATTEND_END + ["zT:1", "logits:1", "gT:1", "fin:1"]

AT = {"uT3": 1, "norm3": 1, "aT": 3, "y": 5, "stats:1": 5, "z:1": 8, "zT:1": 10,
      "xlo:1": 10, "logits:1": 12, "gate_exp:1": 13, "gT:1": 28,
      "fin:0": 37, "stats:a": 37, "n:a": 39, "nT": 40, "qkv0": 41, "qkv1": 42, "rope": 42,
      "split": 47, "kT": 49, "qT0": 50, "qT1": 52, "qT2": 54, "qT3": 56}
GATES_FROM = 14
MAX_FROM = 2 * FFN_CHUNKS - NMAX


class Place:

    def __init__(self, turn, hold, links=(0, 0)):
        self.turn = turn
        self.hold = hold
        self.chunk = hold(turn * (2 * FFN_CHUNKS) + FFN_CHUNKS)
        self.unit = hold(turn * (2 * EXPERTS) + EXPERTS)
        self.ffn = hold(turn * 2 + 1)
        self.added = hold(turn * (2 * (EXPERTS - 1)) + (EXPERTS - 1))
        self.att = hold(turn * 1)
        self.groups = hold(turn * GROUPS)
        self.tiles = hold(turn * (GROUPS * TILES))
        self.scores = hold(turn * (2 * GROUPS * TILES))
        self.maxes = hold(turn * (GROUPS * NMAX))
        self.misc = hold(turn * len(MISC_TURN) + len(MISC_FIRST))
        self.next_att = hold(turn * 1 + 1)
        self.stats = hold(turn * 3 + 2)
        self.next_maxes = hold(turn * (GROUPS * NMAX) + GROUPS * NMAX)
        self.nth = {"0": 0, "1": 1, "a": 2}
        self.links = hold(turn * links[1] + links[0])
        self.first_kind = 0
        self.names = MISC_TURN


class First(Place):

    def __init__(self):
        self.turn = -1
        self.chunk = self.unit = self.ffn = self.added = self.att = self.groups = 0
        self.tiles = self.scores = self.maxes = self.misc = self.stats = self.links = 0
        self.first_kind = 0
        self.next_att = self.next_maxes = 0
        self.nth = {"0": 0, "a": 1}
        self.names = MISC_FIRST


class Last(Place):

    def __init__(self, links=(0, 0)):
        super().__init__(TURNS, lambda value: value, links)
        self.first_kind = 1
        self.nth = {"1": 0}
        self.names = MISC_LAST


POOL_LINKS = (12, 14)
DVE_LINKS = (41, 88)


CONST_LOADS = 15


def counted(found, stated, name):
    assert found == stated, f"{name}: {found}, not {stated}"


def build(nc, x, wq, wk, wv, wo, gamma, beta, Wg, W1, b1, W2, b2,
          ident_d, mask_d, maskT_d, rope_d, rank_d, pick_d, out):
    with ExitStack() as ctx:
        def sb(name, shape, dt=F32):
            return ctx.enter_context(nc.sbuf_tensor(name, shape, dt))

        def sem(name):
            return ctx.enter_context(nc.semaphore(name))

        psum = ctx.enter_context(nc.psum_tensor("psum", [P, 8, 512], F32))

        ident = sb("ident", [P, P])
        ident16 = sb("ident16", [P, P], BF16)
        mask_f = sb("mask_f", [P, 2, P])
        mask16 = sb("mask16", [P, 2, KV, P], BF16)
        rope = sb("rope", [P, TILES, 2, HALF])
        spare = sb("spare", [P, 1])
        rank = sb("rank", [P, EXPERTS])
        pick_f = sb("pick_f", [2 * EXPERTS, EXPERTS, P])
        pick = sb("pick", [2 * EXPERTS, EXPERTS, P], F32R)
        eps = sb("eps", [P, TILES])
        power = sb("power", [P, TILES])
        small = sb("small", [50, P])
        smallT = sb("smallT", [P, 50])
        w1_hi = sb("w1_hi", [P, EXPERTS, F], F32R)
        w1_lo = sb("w1_lo", [P, EXPERTS, F], F32R)
        w2_hi = sb("w2_hi", [P, EXPERTS, CHUNKS, D], F32R)
        w2_lo = sb("w2_lo", [P, EXPERTS, CHUNKS, D], F32R)
        wqkv = sb("wqkv", [P, QKV])
        wo_s = sb("wo_s", [P, D])
        b1T = smallT[:, 0:32]
        b2T = smallT[:, 32:40]
        WgT = smallT[:, 40:48]
        gammaT = smallT[:, 48:49]
        betaT = smallT[:, 49:50]
        x_in = sb("x_in", [P, TILES, D])
        x1 = sb("x1", [P, TILES, D])
        x2 = sb("x2", [P, TILES, D])
        x_out = sb("x_out", [P, TILES, D])
        stats = sb("stats", [P, TILES, 6])
        mv = sb("mv", [P, TILES, 2])
        vt = sb("vt", [P, 6, TILES])
        nrm = sb("nrm", [P, TILES, D])
        z = sb("z", [P, TILES, D])
        res = [sb(f"res{k}", [P, TILES, D]) for k in range(2)]
        xn = sb("xn", [P, S])
        xn_hi = [sb(f"xn_hi{k}", [P, S], F32R) for k in range(2)]
        xn_lo = [sb(f"xn_lo{k}", [P, S], F32R) for k in range(2)]
        gs = sb("gs", [P, 10, TILES, EXPERTS])
        gr = sb("gr", [P, 8, TILES])
        gaug = sb("gaug", [P, TILES, 2 * EXPERTS])
        gT = [sb(f"gT{k}", [2 * EXPERTS, S], F32R) for k in range(2)]
        h = sb("h", [P, CHUNKS, S])
        h_hi = sb("h_hi", [P, CHUNKS, S], F32R)
        h_lo = sb("h_lo", [P, CHUNKS, S], F32R)
        gate = sb("gate", [P, 2, S])
        part = sb("part", [P, 2, S])
        acc = [sb(f"acc{k}", [P, S]) for k in range(2)]
        qk = sb("qk", [P, TILES, QK])
        turned = sb("turned", [P, 4, TILES, ROPED, HALF])
        rot = sb("rot", [P, TILES, ROPED, HD])
        aug = sb("aug", [P, TILES, ROPED, SLOT])
        v = sb("v", [P, TILES, KV, SLOT])
        kT = sb("kT", [P, KV, S], F32R)
        qT = sb("qT", [P, GROUPS, S], F32R)
        q2T = sb("q2T", [P, 2, S], F32R)
        negmax = sb("negmax", [P, TILES, HEADS])
        probs = sb("probs", [P, 2, KV, S])
        arrived = probs[:].rearrange("p a h s -> p (a h) s")

        def w1_f(e):
            return arrived[:, 2 * (e % 4)]

        def w2_f(e):
            return arrived[:, 2 * (e % 4) + 1]

        u = sb("u", [P, S])
        rden = sb("rden", [P, TILES, KV])
        na = ao = z
        nT = aoT = u

        const_loaded = sem("const_loaded")
        expert_loaded = [sem(f"expert_loaded{e}") for e in range(EXPERTS)]
        x_loaded = sem("x_loaded")
        x_out_free = sem("x_out_free")
        ones_set = sem("ones_set")
        consts_cast = sem("consts_cast")
        small_turned = sem("small_turned")
        small_ready = sem("small_ready")
        w_hi_ready = sem("w_hi_ready")
        w_lo_ready = sem("w_lo_ready")
        dve_link = sem("dve_link")
        pool_link = sem("pool_link")
        stats_ready = sem("stats_ready")
        scale_ready = sem("scale_ready")
        z_ready = sem("z_ready")
        res_ready = sem("res_ready")
        xn_ready = sem("xn_ready")
        gates_ready = sem("gates_ready")
        n_ready = sem("n_ready")
        rotated = sem("rotated")
        aug_ready = sem("aug_ready")
        misc_full = sem("misc_full")
        misc_taken = sem("misc_taken")
        gate_exp = sem("gate_exp")
        up_done = sem("up_done")
        down_done = sem("down_done")
        gate_spread = sem("gate_spread")
        gate_copied = sem("gate_copied")
        gelu_done = sem("gelu_done")
        split_done = sem("split_done")
        scaled = sem("scaled")
        added = sem("added")
        max_full = sem("max_full")
        max_taken = sem("max_taken")
        max_split = sem("max_split")
        scores_full = sem("scores_full")
        exp_done = sem("exp_done")
        pv_done = sem("pv_done")
        u_copied = sem("u_copied")

        block = ctx.enter_context(nc.Block())

        def misc(n=512):
            return psum[:, MISC_BANK, 0:n]

        def misc_at(p, name):
            return p.misc + p.names.index(name)

        def wait(eng, s, value):
            if not isinstance(value, int) or value > 0:
                eng.wait_ge(s, value)

        def hooks(steps, m, p):
            for name, step in steps.items():
                if AT[name] == m:
                    step(p)

        def heads_of(t, g):
            return t[:, :, g * KV:(g + 1) * KV, :]

        @block.sync
        def _(sp):
            def load(seq):
                sp.dma_start(x_in[:], x[seq].rearrange("(i p) d -> p i d", p=P)).then_inc(x_loaded, 16)

            def store(seq):
                sp.dma_start(out[seq].rearrange("(i p) d -> p i d", p=P), x_out[:]).then_inc(x_out_free, 16)

            load(0)
            for dst, src in ((small[0:32], b1.rearrange("e (c p) -> (e c) p", p=P)), (small[32:40], b2),
                             (small[40:48], Wg), (small[48:49], gamma[None, :]),
                             (small[49:50], beta[None, :]), (rank[:], rank_d), (pick_f[:], pick_d)):
                sp.dma_start(dst, src).then_inc(const_loaded, 16)
            for e in range(EXPERTS):
                if e >= 4:
                    sp.wait_ge(w_lo_ready, e - 3)
                sp.dma_start(w1_f(e), W1[e]).then_inc(expert_loaded[e], 16)
                sp.dma_start(w2_f(e).rearrange("p (c d) -> p c d", c=CHUNKS),
                             W2[e].rearrange("(c p) d -> p c d", p=P)).then_inc(expert_loaded[e], 16)
            sp.wait_ge(res_ready, 1)
            load(1)
            with sp.Fori(0, TURNS - 1) as turn:
                p = Place(turn, sp.snap)
                sp.wait_ge(res_ready, p.ffn + 1)
                load(turn + 2)
                sp.wait_ge(misc_taken, misc_at(p, "fin:1") + 1)
                store(turn)
            p = Place(TURNS - 1, int)
            sp.wait_ge(misc_taken, misc_at(p, "fin:1") + 1)
            store(TURNS - 1)
            p = Last()
            sp.wait_ge(misc_taken, misc_at(p, "fin:1") + 1)
            store(TURNS)
            sp.wait_ge(x_out_free, 16 + 16 * SEQS)

        @block.gpsimd
        def _(pool):
            at = [0]
            base = [0]

            def link(ins):
                at[0] += 1
                ins.then_inc(pool_link, 1)
                pool.wait_ge(pool_link, base[0] + at[0])

            for ins in (pool.memset(eps[:], EPS), pool.memset(power[:], -0.5), pool.memset(aug[:], 0.0),
                        pool.memset(v[:], 0.0)):
                link(ins)
            pool.memset(kT[:].bitcast(F32), 0.0)
            pool.memset(x_out[:], 0.0).then_inc(x_out_free, 16)
            pool.memset(aug[:, :, HEADS:ROPED, STACK:STACK + 2], 1.0)
            pool.memset(v[:, :, :, HD:HD + 1], 1.0).then_inc(ones_set, 1)

            def norm_scale(p, nth):
                wait(pool, stats_ready, p.stats + p.nth[nth] + 1)
                t = [vt[:, k] for k in range(6)]
                link(pool.tensor_tensor(t[0], mv[:, :, 1], eps[:], ALU.add))
                r = pool.tensor_tensor(t[1], t[0], power[:], ALU.pow)
                if nth != "a":
                    link(r)
                    link(pool.tensor_tensor(t[2], t[1], t[1], ALU.mult))
                    link(pool.tensor_tensor(t[3], t[2], mv[:, :, 1], ALU.mult))
                    link(pool.tensor_tensor(t[4], t[3], eps[:], ALU.add))
                    link(pool.tensor_tensor(t[2], t[4], power[:], ALU.pow))
                    r = pool.tensor_tensor(t[5], t[2], t[1], ALU.mult)
                r.then_inc(scale_ready, 1)

            def rotate(p):
                wait(pool, misc_taken, misc_at(p, "qkv1") + 1)
                t = qk[:].rearrange("p i (h a c) -> p i h a c", a=2, c=HALF)
                for n, (a, b) in enumerate(((0, 0), (1, 1), (0, 1), (1, 0))):
                    cs = rope[:, :, b, None, :].broadcast_to([P, TILES, ROPED, HALF])
                    ins = pool.tensor_tensor(turned[:, n], t[:, :, :, a, :], cs, ALU.mult)
                link(ins)
                pool.tensor_tensor(rot[:, :, :, 0:HALF], turned[:, 0], turned[:, 1], ALU.subtract)
                pool.tensor_tensor(rot[:, :, :, HALF:HD], turned[:, 2], turned[:, 3], ALU.add)\
                    .then_inc(rotated, 1)

            def add(p, n):
                k, e = n // EXPERTS, n % EXPERTS
                if e == 0:
                    return
                sums = p.added + (EXPERTS - 1) * k
                total = acc[k + p.first_kind]
                wait(pool, scaled, p.unit + n + 1)
                if e == 1:
                    pool.tensor_tensor(total[:], part[:, 0], part[:, 1], ALU.add).then_inc(added, 1)
                else:
                    wait(pool, added, sums + (e - 1))
                    pool.tensor_tensor(total[:], total[:], part[:, e % 2], ALU.add).then_inc(added, 1)

            def ffns(p, count, steps):
                for m in range(count * FFN_CHUNKS):
                    if m >= LAG and (m - LAG) % CHUNKS == CHUNKS - 1:
                        add(p, (m - LAG) // CHUNKS)
                    hooks(steps, m, p)
                add(p, count * EXPERTS - 1)

            p = First()
            norm_scale(p, "0")
            ffns(p, 1, {})
            norm_scale(p, "a")
            rotate(p)
            counted(at[0], POOL_LINKS[0], "POOL_LINKS, first")
            with pool.Fori(0, TURNS) as turn:
                p = Place(turn, pool.snap, POOL_LINKS)
                at[0], base[0] = 0, p.links
                norm_scale(p, "0")
                ffns(p, 2, {"stats:1": lambda p: norm_scale(p, "1"),
                            "stats:a": lambda p: norm_scale(p, "a"), "rope": rotate})
                counted(at[0], POOL_LINKS[1], "POOL_LINKS")
            p = Last(POOL_LINKS)
            at[0], base[0] = 0, p.links
            norm_scale(p, "1")
            ffns(p, 1, {})

        @block.scalar
        def _(act):
            for dst, src in ((ident[:], ident_d), (mask_f[:, 0], mask_d), (mask_f[:, 1], maskT_d),
                             (rope[:], rope_d), (wqkv[:, 0:D], wq), (wqkv[:, D:D + KV * HD], wk),
                             (wqkv[:, QK:QKV], wv), (wo_s[:], wo)):
                act.dma_start(dst, src).then_inc(const_loaded, 16)
            act.wait_ge(small_turned, 1)
            act.activation(smallT[:], misc(50), ACT.Copy).then_inc(small_ready, 1)
            act.wait_ge(small_ready, 1)
            act.wait_ge(ones_set, 1)

            def weights_hi(e):
                act.wait_ge(expert_loaded[e], 32)
                act.activation(w1_hi[:, e], w1_f(e), ACT.Copy)
                act.activation(w2_hi[:, e].rearrange("p c d -> p (c d)"), w2_f(e), ACT.Copy).then_inc(w_hi_ready, 1)

            def take(p, name, *pairs):
                wait(act, misc_full, misc_at(p, name) + 1)
                for dst, src in pairs:
                    ins = act.activation(dst, src, ACT.Copy)
                ins.then_inc(misc_taken, 1)

            def take_z(p, k):
                wait(act, misc_full, misc_at(p, f"zT:{k}") + 1)
                wait(act, xn_ready, p.ffn + (k - p.first_kind))
                act.activation(xn[:], misc(), ACT.Identity, bias=betaT, scale=gammaT)
                act.activation(xn_hi[k][:], misc(), ACT.Identity, bias=betaT, scale=gammaT)\
                   .then_inc(misc_taken, 1)

            def exp_gate(p, k):
                wait(act, misc_taken, misc_at(p, f"logits:{k}") + 1)
                act.activation(gs[:, 1], gs[:, 0], ACT.Exp).then_inc(gate_exp, 1)

            def take_gates(p, k):
                take(p, f"gT:{k}", (gT[k][:], psum[0:2 * EXPERTS, MISC_BANK, :]))

            def take_qkv(p, half):
                src = misc(2 * QKV).rearrange("p (i c) -> p i c", i=2)
                t = slice(2 * half, 2 * half + 2)
                wait(act, misc_full, misc_at(p, f"qkv{half}") + 1)
                for i in range(2):
                    act.activation(v[:, 2 * half + i, :, 0:HD],
                                   src[:, i, QK:QKV].rearrange("p (h d) -> p h d", h=KV), ACT.Copy)
                act.activation(qk[:, t], src[:, :, 0:QK], ACT.Copy).then_inc(misc_taken, 1)

            def gelu(p, m):
                e, c = m // CHUNKS % EXPERTS, m % CHUNKS
                wait(act, up_done, p.chunk + m + 1)
                wait(act, split_done, p.chunk + (m - CHUNKS + 1))
                bias = b1T[:, CHUNKS * e + c:CHUNKS * e + c + 1]
                if c % 2:
                    wait(act, down_done, p.chunk + (m - CHUNKS + 1))
                    act.activation(h_hi[:, c], psum[:, UP_BANK + m % 2], ACT.Gelu_apprx_tanh, bias=bias)
                act.activation(h[:, c], psum[:, UP_BANK + m % 2], ACT.Gelu_apprx_tanh, bias=bias)\
                   .then_inc(gelu_done, 1)

            def copy_gate(p, n):
                wait(act, gate_spread, p.unit + n + 1)
                wait(act, scaled, p.unit + (n - 1))
                act.activation(gate[:, n % 2], psum[:, GATE_BANK], ACT.Copy).then_inc(gate_copied, 1)

            def ffns(p, count, steps, first=False):
                for m in range(count * FFN_CHUNKS):
                    if first and m % CHUNKS == 0 and m // CHUNKS + 2 < EXPERTS:
                        weights_hi(m // CHUNKS + 2)
                    gelu(p, m)
                    if m % CHUNKS == 0:
                        copy_gate(p, m // CHUNKS)
                    hooks(steps, m, p)

            def copy_u(p, g):
                wait(act, pv_done, p.tiles + TILES * (g + 1))
                if g > 0:
                    wait(act, misc_full, misc_at(p, f"uT{g - 1}") + 1)
                act.activation(u[:], psum[:, PV_BANK], ACT.Copy).then_inc(u_copied, 1)

            def take_q2(p, g):
                take(p, f"q2T{g}", (q2T[:, g % 2], misc()))

            def take_o(p):
                take(p, "aT", (aoT[:], misc()))

            def attend(p, prepares):
                take_q2(p, 0)
                for g in range(GROUPS):
                    for j in range(TILES):
                        for pair in range(2):
                            s, n = 2 * (TILES * g + j) + pair, S - P * j
                            wait(act, scores_full, p.scores + s + 1)
                            if TILES * g + j >= 2:
                                wait(act, pv_done, p.tiles + (TILES * g + j - 1))
                            b = SCORE_BANK + 2 * pair
                            act.activation(probs[:, j % 2, 2 * pair:2 * pair + 2, 0:n],
                                           psum[:, b:b + 2, 0:n], ACT.Exp, scale=SCALE)\
                               .then_inc(exp_done, 1)
                        if j == 0 and g > 0:
                            copy_u(p, g - 1)
                        if j == 0 and g == 1 and prepares:
                            take_z(p, 0)
                        if g < GROUPS - 1 and j == (3 if g == 2 else 2):
                            take_q2(p, g + 1)
                        if j == 0 and g == 2 and prepares:
                            exp_gate(p, 0)
                    if g == GROUPS - 1 and prepares:
                        take_gates(p, 0)
                copy_u(p, GROUPS - 1)

            after = {"nT": lambda p: take(p, "nT", (nT[:], misc())),
                     "qkv0": lambda p: take_qkv(p, 0), "qkv1": lambda p: take_qkv(p, 1),
                     "kT": lambda p: take(p, "kT", *[(kT[SLOT * kv:SLOT * (kv + 1), kv],
                                                      psum[SLOT * kv:SLOT * (kv + 1), MISC_BANK, :])
                                                     for kv in range(KV)])}
            for g in range(GROUPS):
                after[f"qT{g}"] = lambda p, g=g: take(p, f"qT{g}", (qT[:, g], misc()))
            between = {"aT": take_o,
                       "zT:1": lambda p: take_z(p, 1), "gate_exp:1": lambda p: exp_gate(p, 1),
                       "gT:1": lambda p: take_gates(p, 1)}

            p = First()
            weights_hi(0)
            weights_hi(1)
            take_z(p, 0)
            exp_gate(p, 0)
            take_gates(p, 0)
            ffns(p, 1, {}, first=True)
            for step in after.values():
                step(p)
            with act.Fori(0, TURNS) as turn:
                p = Place(turn, act.snap)
                attend(p, True)
                ffns(p, 2, between | after)
            p = Last()
            attend(p, False)
            for step in between.values():
                step(p)
            ffns(p, 1, {})

        @block.vector
        def _(dve):
            at = [0]
            base = [0]

            def link(ins):
                at[0] += 1
                ins.then_inc(dve_link, 1)
                dve.wait_ge(dve_link, base[0] + at[0])

            def along(col, n):
                return col[:, :, None].broadcast_to([P, TILES, n])

            def weights_lo(e):
                dve.wait_ge(w_hi_ready, e + 1)
                dve.tensor_tensor(w1_lo[:, e], w1_f(e), w1_hi[:, e].bitcast(F32), ALU.subtract)
                dve.tensor_tensor(w2_lo[:, e].rearrange("p c d -> p (c d)"), w2_f(e),
                                  w2_hi[:, e].rearrange("p c d -> p (c d)").bitcast(F32), ALU.subtract)\
                   .then_inc(w_lo_ready, 1)

            def statistics(src):
                for i in range(TILES):
                    ins = dve.bn_stats(stats[:, i], src[:, i])
                link(ins)
                dve.memset(spare[:], 0.0)
                for i in range(TILES):
                    ins = dve.bn_aggr(mv[:, i], stats[:, i])
                ins.then_inc(stats_ready, 1)

            def normalize(dst, src, scale):
                for i in range(TILES):
                    ins = dve.tensor_scalar(dst[:, i], src[:, i], mv[:, i, 0:1], scale[:, i:i + 1],
                                            ALU.subtract, ALU.mult)
                return ins

            def make_z(p, k, src):
                wait(dve, scale_ready, p.stats + p.nth[str(k)] + 1)
                link(normalize(nrm, src, vt[:, 1]))
                normalize(z, src, vt[:, 5]).then_inc(z_ready, 1)
                dve.scalar_tensor_tensor(res[k][:], nrm[:], 0.5, src[:], ALU.mult, ALU.add)\
                   .then_inc(res_ready, 1)

            def make_xlo(p, k):
                wait(dve, misc_taken, misc_at(p, f"zT:{k}") + 1)
                dve.tensor_tensor(xn_lo[k][:], xn[:], xn_hi[k][:].bitcast(F32), ALU.subtract)\
                   .then_inc(xn_ready, 1)

            def shift_logits(p, k):
                wait(dve, misc_full, misc_at(p, f"logits:{k}") + 1)
                logits = misc(TILES * EXPERTS).rearrange("p (i e) -> p i e", i=TILES)
                link(dve.tensor_reduce(gr[:, 0], logits, AX_X, ALU.max))
                dve.tensor_tensor(gs[:, 0], logits, along(gr[:, 0], EXPERTS), ALU.subtract)\
                   .then_inc(misc_taken, 1)

            def make_gates(p, k):
                _, ex, pr, eq, one1, left, one2, both, share, ranked = [gs[:, n] for n in range(10)]
                top0, total, inverse, top1, top2, best, sum2, inverse2 = [gr[:, n] for n in range(8)]
                ranks = rank[:, None, :].broadcast_to([P, TILES, EXPERTS])
                hi = gaug[:, :, 0:EXPERTS]

                def pick_largest(values, top, one):
                    yield lambda: dve.tensor_reduce(top, values, AX_X, ALU.max)
                    yield lambda: dve.tensor_tensor(eq, values, along(top, EXPERTS), ALU.is_equal)
                    yield lambda: dve.tensor_tensor(ranked, eq, ranks, ALU.mult)
                    yield lambda: dve.tensor_reduce(best, ranked, AX_X, ALU.max)
                    yield lambda: dve.tensor_tensor(one, ranks, along(best, EXPERTS), ALU.is_equal)

                yield lambda: dve.tensor_reduce(total, ex, AX_X, ALU.add)
                yield lambda: dve.reciprocal(inverse, total)
                yield lambda: dve.tensor_tensor(pr, ex, along(inverse, EXPERTS), ALU.mult)
                yield from pick_largest(pr, top1, one1)
                yield lambda: dve.scalar_tensor_tensor(left, one1, -2.0, pr, ALU.mult, ALU.add)
                yield from pick_largest(left, top2, one2)
                yield lambda: dve.scalar_tensor_tensor(sum2, top1, GATE_EPS, top2, ALU.add, ALU.add)
                yield lambda: dve.reciprocal(inverse2, sum2)
                yield lambda: dve.tensor_tensor(both, one1, one2, ALU.add)
                yield lambda: dve.tensor_tensor(both, both, pr, ALU.mult)
                yield lambda: dve.tensor_tensor(share, both, along(inverse2, EXPERTS), ALU.mult)
                yield lambda: dve.tensor_copy(hi.bitcast(F32R), share)
                yield lambda: dve.tensor_tensor(gaug[:, :, EXPERTS:2 * EXPERTS], share, hi, ALU.subtract)

            def gate_steps(p, k):
                reached = None
                steps = list(make_gates(p, k))
                for n, step in enumerate(steps):
                    if reached is None:
                        wait(dve, gate_exp, p.ffn + (k - p.first_kind) + 1)
                    else:
                        dve.wait_ge(dve_link, reached)
                    if n < len(steps) - 1:
                        at[0] += 1
                        reached = base[0] + at[0]
                        step().then_inc(dve_link, 1)
                    else:
                        step().then_inc(gates_ready, 1)
                    yield

            def round_h(p, m):
                c = m % CHUNKS
                wait(dve, gelu_done, p.chunk + m + 1)
                wait(dve, down_done, p.chunk + (m - CHUNKS + 1))
                at[0] += 1
                dve.tensor_copy(h_hi[:, c], h[:, c]).then_inc(dve_link, 1)
                return base[0] + at[0]

            def rest_h(p, m, rounded=None):
                c = m % CHUNKS
                if rounded is None:
                    wait(dve, gelu_done, p.chunk + m + 1)
                    wait(dve, down_done, p.chunk + (m - CHUNKS + 1))
                else:
                    dve.wait_ge(dve_link, rounded)
                dve.tensor_tensor(h_lo[:, c], h[:, c], h_hi[:, c].bitcast(F32), ALU.subtract)\
                   .then_inc(split_done, 1)

            def split(p, m):
                if m % 2 == 0:
                    rounded = round_h(p, m)
                    if m > 0:
                        rest_h(p, m - 1)
                    rest_h(p, m, rounded)

            def scale(p, n):
                e = n % EXPERTS
                sums = p.added + (EXPERTS - 1) * (n // EXPERTS)
                wait(dve, down_done, p.chunk + CHUNKS * (n + 1))
                wait(dve, gate_copied, p.unit + n + 1)
                wait(dve, added, sums + (max(e - 2, 1) if e > 1 else 0))
                dve.scalar_tensor_tensor(part[:, e % 2], psum[:, Y_BANK + n % 2], b2T[:, e:e + 1],
                                         gate[:, n % 2], ALU.add, ALU.mult).then_inc(scaled, 1)

            def ffns(p, count, steps, first=False):
                gate = gate_steps(p, 1)
                for m in range(count * FFN_CHUNKS):
                    if first and m % CHUNKS == 0 and m // CHUNKS + 2 < EXPERTS:
                        weights_lo(m // CHUNKS + 2)
                    split(p, m)
                    if m >= LAG and (m - LAG) % CHUNKS == CHUNKS - 1:
                        scale(p, (m - LAG) // CHUNKS)
                    hooks(steps, m, p)
                    if count == 2 and GATES_FROM <= m:
                        for _ in range(2):
                            next(gate, None)
                    if m >= MAX_FROM:
                        for block in range(2 * (m - MAX_FROM), 2 * (m - MAX_FROM) + 2):
                            take_max(p.next_maxes, block)
                rest_h(p, count * FFN_CHUNKS - 1)
                scale(p, count * EXPERTS - 1)

            def finish(p, k, dst):
                wait(dve, misc_full, misc_at(p, f"fin:{k}") + 1)
                if k == 1:
                    wait(dve, x_out_free, p.turn * 16 + 16)
                ins = dve.scalar_tensor_tensor(dst[:].rearrange("p i d -> p (i d)"), misc(), 0.5,
                                               res[k][:].rearrange("p i d -> p (i d)"), ALU.mult, ALU.add)
                ins.then_inc(misc_taken, 1)
                dve.wait_ge(misc_taken, misc_at(p, f"fin:{k}") + 1)

            def norm_for_attention(p):
                wait(dve, scale_ready, p.stats + p.nth["a"] + 1)
                normalize(na, x1, vt[:, 1]).then_inc(n_ready, 1)

            def stack(p):
                wait(dve, rotated, p.next_att + 1)
                for h0, h1, his, lo in ((0, HEADS, (0, HD), 2 * HD), (HEADS, ROPED, (0, 2 * HD), HD)):
                    for a in his:
                        ins = dve.tensor_copy(aug[:, :, h0:h1, a:a + HD].bitcast(F32R), rot[:, :, h0:h1])
                dve.memset(aug[:, :, 0:HEADS, STACK:STACK + 2], 0.0)
                link(ins)
                for h0, h1, his, lo in ((0, HEADS, (0, HD), 2 * HD), (HEADS, ROPED, (0, 2 * HD), HD)):
                    ins = dve.tensor_tensor(aug[:, :, h0:h1, lo:lo + HD], rot[:, :, h0:h1],
                                            aug[:, :, h0:h1, 0:HD], ALU.subtract)
                ins.then_inc(aug_ready, 1)

            def take_max(maxes, at):
                g, (tile, heads) = at // NMAX, MAX_BLOCKS[at % NMAX]
                n, h0 = P * (tile + 1), g * KV + heads[0]
                wait(dve, max_full, maxes + at + 1)
                src = psum[:, MAX_BANK + at % 2, 0:n * len(heads)].rearrange("p (h n) -> p h n", n=n)
                dve.tensor_reduce(negmax[:, tile, h0:h0 + len(heads)], src, AX_X, ALU.max, negate=True)\
                   .then_inc(max_taken, 1)

            def split_max(p, g):
                wait(dve, max_taken, p.maxes + NMAX * (g + 1))
                heads = slice(g * KV, (g + 1) * KV)
                src = negmax[:, :, heads, None]
                hi = heads_of(aug, g)[:, :, :, STACK:STACK + 1]
                link(dve.tensor_copy(hi.bitcast(F32R), src))
                dve.tensor_tensor(heads_of(aug, g)[:, :, :, STACK + 1:STACK + 2], src, hi, ALU.subtract)\
                   .then_inc(max_split, 1)

            def divide(p, g):
                wait(dve, misc_full, misc_at(p, f"uT{g}") + 1)
                src = misc().rearrange("p (i h c) -> p i h c", i=TILES, h=KV)
                link(dve.reciprocal(rden[:], src[:, :, :, HD]))
                dst = ao[:].rearrange("p i (g h d) -> p i g h d", g=GROUPS, h=KV)[:, :, g]
                dve.tensor_tensor(dst, src[:, :, :, 0:HD],
                                  rden[:, :, :, None].broadcast_to([P, TILES, KV, HD]), ALU.mult)\
                   .then_inc(misc_taken, 1)

            def attend(p, prepares):
                for g in range(2):
                    split_max(p, g)
                if prepares:
                    dve.wait_ge(x_loaded, (p.turn + 2) * 16)
                    statistics(x_in)
                    gate = gate_steps(p, 0)
                for step in range(2 * TILES * GROUPS):
                    g = step // (2 * TILES)
                    if 2 * NMAX + step < GROUPS * NMAX:
                        take_max(p.maxes, 2 * NMAX + step)
                        if (step + 1) % NMAX == 0:
                            split_max(p, 2 + step // NMAX)
                    if step % (2 * TILES) == 4 and g > 0:
                        divide(p, g - 1)
                    if step == 4 and prepares:
                        make_z(p, 0, x_in)
                    if step == 11 and prepares:
                        make_xlo(p, 0)
                    if step == 16 and prepares:
                        shift_logits(p, 0)
                    if step >= 19 and prepares:
                        for _ in range(2):
                            next(gate, None)
                if prepares:
                    assert next(gate, "all") == "all"

            def add_attention(p):
                wait(dve, misc_full, misc_at(p, "y") + 1)
                dve.tensor_tensor(x2[:].rearrange("p i d -> p (i d)"), misc(),
                                  x1[:].rearrange("p i d -> p (i d)"), ALU.add).then_inc(misc_taken, 1)
                dve.wait_ge(misc_taken, misc_at(p, "y") + 1)

            between = {"norm3": lambda p: divide(p, GROUPS - 1), "y": add_attention,
                       "stats:1": lambda p: statistics(x2), "z:1": lambda p: make_z(p, 1, x2),
                       "xlo:1": lambda p: make_xlo(p, 1), "logits:1": lambda p: shift_logits(p, 1)}
            after = {"fin:0": lambda p: finish(p, 0, x1), "stats:a": lambda p: statistics(x1),
                     "n:a": norm_for_attention, "split": stack}

            dve.wait_ge(const_loaded, 16 * CONST_LOADS)
            dve.tensor_copy(ident16[:], ident[:])
            for kv in range(KV):
                dve.tensor_copy(mask16[:, :, kv], mask_f[:])
            dve.tensor_copy(pick[:], pick_f[:]).then_inc(consts_cast, 1)
            p = First()
            dve.wait_ge(x_loaded, 16)
            statistics(x_in)
            make_z(p, 0, x_in)
            dve.wait_ge(small_ready, 1)
            make_xlo(p, 0)
            shift_logits(p, 0)
            for _ in gate_steps(p, 0):
                pass
            weights_lo(0)
            weights_lo(1)
            ffns(p, 1, {}, first=True)
            for step in after.values():
                step(p)
            for block in range(2 * NMAX):
                take_max(p.next_maxes, block)
            counted(at[0], DVE_LINKS[0], "DVE_LINKS, first")
            with dve.Fori(0, TURNS) as turn:
                p = Place(turn, dve.snap, DVE_LINKS)
                at[0], base[0] = 0, p.links
                attend(p, True)
                ffns(p, 2, between | after)
                finish(p, 1, x_out)
                counted(at[0], DVE_LINKS[1], "DVE_LINKS, turn")
            p = Last(DVE_LINKS)
            at[0], base[0] = 0, p.links
            attend(p, False)
            for step in between.values():
                step(p)
            for _ in gate_steps(p, 1):
                pass
            ffns(p, 1, {})
            finish(p, 1, x_out)

        @block.tensor
        def _(pe):
            mm = nc.tensor.matmul

            def use_misc(p, name):
                wait(pe, misc_taken, misc_at(p, name))

            def turn_tiles(p, name, parts, rows=P):
                use_misc(p, name)
                for i, part_i in enumerate(parts):
                    ins = nc.tensor.transpose(psum[0:rows, MISC_BANK, i * P:(i + 1) * P], part_i, ident[:])
                ins.then_inc(misc_full, 1)

            def turn_z(p, k):
                wait(pe, z_ready, p.ffn + (k - p.first_kind) + 1)
                turn_tiles(p, f"zT:{k}", [z[:, i] for i in range(TILES)])

            def make_logits(p, k):
                use_misc(p, f"logits:{k}")
                for i in range(TILES):
                    ins = mm(psum[:, MISC_BANK, i * EXPERTS:(i + 1) * EXPERTS], xn[:, i * P:(i + 1) * P],
                             WgT, start=True, stop=True)
                ins.then_inc(misc_full, 1)

            def turn_gates(p, k):
                wait(pe, gates_ready, p.ffn + (k - p.first_kind) + 1)
                turn_tiles(p, f"gT:{k}", [gaug[:, i] for i in range(TILES)], 2 * EXPERTS)

            def up(p, m, first):
                n, e, c = m // CHUNKS, m // CHUNKS % EXPERTS, m % CHUNKS
                k = n // EXPERTS + p.first_kind
                if m % FFN_CHUNKS == 0:
                    wait(pe, xn_ready, p.ffn + (k - p.first_kind) + 1)
                if first and c == 0:
                    pe.wait_ge(w_lo_ready, e + 1)
                wait(pe, gelu_done, p.chunk + (m - 1))
                o, cols = psum[:, UP_BANK + m % 2], slice(c * P, (c + 1) * P)
                mm(o, w1_hi[:, e, cols], xn_hi[k][:], start=True, stop=False)
                mm(o, w1_hi[:, e, cols], xn_lo[k][:], start=False, stop=False)
                mm(o, w1_lo[:, e, cols], xn_hi[k][:], start=False, stop=True).then_inc(up_done, 1)
                if c == 0:
                    wait(pe, gate_copied, p.unit + n)
                    if e == 0:
                        wait(pe, misc_taken, misc_at(p, f"gT:{k}") + 1)
                    if n == 0 and not isinstance(p, First):
                        wait(pe, u_copied, p.groups + GROUPS)
                    mm(psum[:, GATE_BANK], pick[:, e], gT[k][:], start=True, stop=True)\
                        .then_inc(gate_spread, 1)

            def down(p, m):
                n, e, c = m // CHUNKS, m // CHUNKS % EXPERTS, m % CHUNKS
                wait(pe, split_done, p.chunk + m + 1)
                if c == 0:
                    wait(pe, scaled, p.unit + (n - 1))
                o = psum[:, Y_BANK + n % 2]
                mm(o, w2_hi[:, e, c], h_hi[:, c], start=(c == 0), stop=False)
                mm(o, w2_hi[:, e, c], h_lo[:, c], start=False, stop=False)
                mm(o, w2_lo[:, e, c], h_hi[:, c], start=False, stop=(c == CHUNKS - 1)).then_inc(down_done, 1)

            def ffns(p, count, steps, first=False):
                for m in range(count * FFN_CHUNKS):
                    up(p, m, first)
                    if m >= LAG:
                        down(p, m - LAG)
                    hooks(steps, m, p)
                    if m >= MAX_FROM:
                        for at in range(2 * (m - MAX_FROM), 2 * (m - MAX_FROM) + 2):
                            if at % NMAX == 0:
                                wait(pe, misc_taken, misc_at(p, f"qT{at // NMAX}") + 1)
                            block_max(p.next_maxes, at)
                for m in range(count * FFN_CHUNKS - LAG, count * FFN_CHUNKS):
                    down(p, m)

            def finish(p, k):
                wait(pe, added, p.added + (EXPERTS - 1) * (k - p.first_kind + 1))
                turn_tiles(p, f"fin:{k}", [acc[k][:, i * P:(i + 1) * P] for i in range(TILES)])

            def turn_n(p):
                wait(pe, n_ready, p.next_att + 1)
                turn_tiles(p, "nT", [na[:, i] for i in range(TILES)])

            def project(p, half):
                use_misc(p, f"qkv{half}")
                for i in range(2):
                    t = 2 * half + i
                    ins = mm(psum[:, MISC_BANK, i * QKV:(i + 1) * QKV], nT[:, t * P:(t + 1) * P], wqkv[:],
                             start=True, stop=True)
                ins.then_inc(misc_full, 1)

            def turn_heads(p, name, h0):
                turn_tiles(p, name, [aug[:, i, h0:h0 + KV].rearrange("p h c -> p (h c)")
                                     for i in range(TILES)])

            def turn_keys(p):
                wait(pe, aug_ready, p.next_att + 1)
                turn_heads(p, "kT", HEADS)

            def block_max(maxes, at):
                g, (tile, heads) = at // NMAX, MAX_BLOCKS[at % NMAX]
                n = P * (tile + 1)
                if at >= 2:
                    wait(pe, max_taken, maxes + (at - 1))
                o = psum[:, MAX_BANK + at % 2, 0:n * len(heads)].rearrange("p (h n) -> p h n", n=n)
                for i, kv in enumerate(heads):
                    mm(o[:, i], qT[:, g, tile * P:(tile + 1) * P], kT[:, kv, 0:n], start=(i == 0), stop=False)
                mm(o[:, :, tile * P:n], ident16[:], mask16[:, 0, 0:len(heads)], start=False, stop=True)\
                    .then_inc(max_full, 1)

            def turn_q2(p, g):
                wait(pe, max_split, p.groups + g + 1)
                turn_heads(p, f"q2T{g}", g * KV)

            def score(p, g, j, pair):
                s, n = 2 * (TILES * g + j) + pair, S - P * j
                if s >= 2:
                    wait(pe, exp_done, p.scores + (s - 1))
                if s % (2 * TILES) == 0:
                    wait(pe, misc_taken, misc_at(p, f"q2T{g}") + 1)
                bank = SCORE_BANK + 2 * pair
                for i in range(2):
                    mm(psum[:, bank + i, 0:n], kT[:, 2 * pair + i, j * P:(j + 1) * P],
                       q2T[:, g % 2, j * P:S], start=True, stop=False)
                for i in range(2):
                    ins = mm(psum[:, bank + i, 0:P], ident16[:], mask16[:, 1, 0], start=False, stop=True)
                ins.then_inc(scores_full, 1)

            def weigh(p, g, j):
                wait(pe, exp_done, p.scores + 2 * (TILES * g + j + 1))
                if j == 0 and g > 0:
                    wait(pe, u_copied, p.groups + g)
                for kv in range(KV):
                    ins = mm(psum[SLOT * kv:SLOT * (kv + 1), PV_BANK, j * P:S], v[:, j, kv],
                             probs[:, j % 2, kv, 0:S - P * j], start=(j == 0), stop=(j == TILES - 1))
                ins.then_inc(pv_done, 1)

            def turn_u(p, g):
                wait(pe, u_copied, p.groups + g + 1)
                turn_tiles(p, f"uT{g}", [u[:, i * P:(i + 1) * P] for i in range(TILES)])

            def turn_o(p):
                turn_tiles(p, "aT", [ao[:, i] for i in range(TILES)])

            def project_o(p):
                use_misc(p, "y")
                for i in range(TILES):
                    ins = mm(psum[:, MISC_BANK, i * D:(i + 1) * D], aoT[:, i * P:(i + 1) * P], wo_s[:],
                             start=True, stop=True)
                ins.then_inc(misc_full, 1)

            def attend(p, prepares):
                turn_q2(p, 0)
                wait(pe, gate_copied, p.unit)
                wait(pe, gelu_done, p.chunk)
                wait(pe, scaled, p.unit)
                for g in range(GROUPS):
                    if g == 1 and prepares:
                        turn_z(p, 0)
                    for j in range(TILES):
                        for pair in range(2):
                            score(p, g, j, pair)
                            ahead = 2 * NMAX + 2 * (TILES * g + j) + pair
                            if ahead < GROUPS * NMAX:
                                block_max(p.maxes, ahead)
                        if g < GROUPS - 1 and j == (3 if g == 2 else 2):
                            turn_q2(p, g + 1)
                        if j > 0:
                            weigh(p, g, j - 1)
                        elif g > 0:
                            weigh(p, g - 1, TILES - 1)
                        if j == 1 and g > 0:
                            turn_u(p, g - 1)
                    if g == 1 and prepares:
                        make_logits(p, 0)
                    if g == GROUPS - 1 and prepares:
                        turn_gates(p, 0)
                weigh(p, GROUPS - 1, TILES - 1)

            between = {"uT3": lambda p: turn_u(p, GROUPS - 1), "aT": turn_o, "y": project_o,
                       "zT:1": lambda p: turn_z(p, 1), "logits:1": lambda p: make_logits(p, 1),
                       "gT:1": lambda p: turn_gates(p, 1)}
            after = {"fin:0": lambda p: finish(p, 0), "nT": turn_n, "qkv0": lambda p: project(p, 0),
                     "qkv1": lambda p: project(p, 1), "kT": turn_keys}
            for g in range(GROUPS):
                after[f"qT{g}"] = lambda p, g=g: turn_heads(p, f"qT{g}", g * KV)

            pe.wait_ge(const_loaded, 16 * CONST_LOADS)
            nc.tensor.transpose(misc(50), small[:], ident[0:50, 0:50]).then_inc(small_turned, 1)
            pe.wait_ge(small_ready, 1)
            pe.wait_ge(consts_cast, 1)
            p = First()
            turn_z(p, 0)
            make_logits(p, 0)
            turn_gates(p, 0)
            ffns(p, 1, {}, first=True)
            for step in after.values():
                step(p)
            wait(pe, misc_taken, misc_at(p, "qT1") + 1)
            for at in range(2 * NMAX):
                block_max(p.next_maxes, at)
            with pe.Fori(0, TURNS) as turn:
                p = Place(turn, pe.snap)
                attend(p, True)
                wait(pe, exp_done, p.scores + 2 * GROUPS * TILES)
                ffns(p, 2, between | after)
                finish(p, 1)
            p = Last()
            attend(p, False)
            for step in between.values():
                step(p)
            wait(pe, exp_done, p.scores + 2 * GROUPS * TILES)
            ffns(p, 1, {})
            finish(p, 1)


NAMES = ["L0_attn_x", "L0_attn_wq", "L0_attn_wk", "L0_attn_wv", "L0_attn_wo", "L0_ffn_gamma",
         "L0_ffn_beta", "L0_ffn_Wg", "L0_ffn_W1", "L0_ffn_b1", "L0_ffn_W2", "L0_ffn_b2"]


def shape_constants():
    f = np.float32
    at = np.arange(P)
    inverse = f(1.0) / f(10000.0) ** (np.arange(HALF, dtype=f) / f(HALF))
    angle = np.arange(S, dtype=f)[:, None] * inverse[None, :]
    rope = np.stack([np.cos(angle), np.sin(angle)], axis=1).astype(f)
    rope = rope.reshape(TILES, P, 2, HALF).transpose(1, 0, 2, 3)
    rank = np.broadcast_to(np.arange(EXPERTS, 0, -1).astype(f), (P, EXPERTS))
    pick = np.zeros((2 * EXPERTS, EXPERTS, P), f)
    for row in range(2 * EXPERTS):
        pick[row, row % EXPERTS] = 1.0
    return {"table_identity": np.eye(P, dtype=f),
            "table_mask": np.where(at[None, :] <= at[:, None], f(0.0), f(MASKED)),
            "table_mask_turned": np.where(at[None, :] >= at[:, None], f(0.0), f(MASKED)),
            "table_rope": rope, "table_rank": rank, "table_pick": pick}


def kernel(**inputs):
    import concourse.bacc as bacc
    from concourse.bass_utils import run_bass_kernel_spmd

    nc = bacc.Bacc("TRN2", target_bir_lowering=False, num_devices=1)
    arrays = {name: np.ascontiguousarray(inputs[name]) for name in NAMES}
    arrays.update({name: np.ascontiguousarray(a) for name, a in shape_constants().items()})
    args = [nc.dram_tensor(name, a.shape, mybir.dt.from_np(a.dtype), kind="ExternalInput").ap()
            for name, a in arrays.items()]
    out = nc.dram_tensor("out", (SEQS, S, D), F32, kind="ExternalOutput").ap()
    build(nc, *args, out)
    return run_bass_kernel_spmd(nc, [arrays], core_ids=[0]).results[0]["out"]
```

```python
from contextlib import ExitStack

import numpy as np

import concourse.bass as bass
from concourse import mybir

F32 = mybir.dt.float32
F32R = mybir.dt.float32r
BF16 = mybir.dt.bfloat16
ALU = mybir.AluOpType
ACT = mybir.ActivationFunctionType
AX_X = mybir.AxisListType.X

P = 128
SEQS, S, D = 8, 512, 128
TILES = S // P
EXPERTS, F = 8, 512
CHUNKS = F // P
HEADS, KV, HD = 16, 4, 8
GROUPS = HEADS // KV
HALF = HD // 2
ROPED = HEADS + KV
SLOT = P // KV
QK = ROPED * HD
QKV = QK + KV * HD
STACK = 3 * HD
EPS = 1e-5
GATE_EPS = 1e-9
MASKED = -1e30
SCALE = float(1.0 / np.sqrt(np.float32(HD)))

FFN_CHUNKS = EXPERTS * CHUNKS
LAG = 3
TURNS = SEQS - 1

UP_BANK, Y_BANK, GATE_BANK, MISC_BANK = 0, 2, 4, 7
SCORE_BANK, PV_BANK, MAX_BANK = 0, 4, 5

MAX_BLOCKS = [(0, (0, 1, 2, 3)), (1, (0, 1)), (1, (2, 3))] + \
             [(tile, (kv,)) for tile in (2, 3) for kv in range(KV)]
NMAX = len(MAX_BLOCKS)

FFN_PREP = ["zT", "logits", "gT"]
ATT_PREP = ["nT", "qkv0", "qkv1", "kT", "qT0", "qT1", "qT2", "qT3"]
ATTEND = ["q2T1", "uT0", "q2T2", "zT:0", "uT1", "q2T3", "logits:0", "uT2", "gT:0"]
ATTEND_END = ["uT3", "aT", "y"]
MISC_FIRST = ["zT:0", "logits:0", "gT:0", "fin:0"] + ATT_PREP + ["q2T0"]
MISC_TURN = ATTEND + ATTEND_END + ["zT:1", "logits:1", "gT:1", "fin:0"] + ATT_PREP + ["q2T0", "fin:1"]
MISC_LAST = [x for x in ATTEND if ":" not in x] + ATTEND_END + ["zT:1", "logits:1", "gT:1", "fin:1"]

AT = {"uT3": 1, "norm3": 2, "aT": 5, "y": 7, "stats:1": 9, "z:1": 11, "res:1": 10, "zT:1": 13, "xlo:1": 13,
      "logits:1": 15, "gate_exp:1": 15, "gT:1": 30,
      "fin:0": 37, "stats:a": 37, "n:a": 39, "nT": 41, "qkv0": 42, "qkv1": 43, "rope": 43, "rotate": 44,
      "stackK": 45, "stackQ": 46, "kT": 47, "qT0": 49, "qT1": 51, "qT2": 53, "qT3": 55, "max0": 59,
      "q2T0": 60}
AT_FIRST = {"gT:0": 4, "spread": 4}
AT_LAST = {"logits:1": 0, "gT:1": 5, "spread": 5}
GATES_FROM = 21
MAX_FROM = 50
AHEAD = 2 * NMAX
BLOCKS_PER_STEP = (2, 2, 2, 1, 1, 1, 1, 0)
THREE_PAIRS_FROM = 20
HEAD_STEPS = 4
SPREAD = 2


def blocks_after(m):
    if m < MAX_FROM:
        return range(0)
    span = 2 * FFN_CHUNKS - MAX_FROM
    return range((m - MAX_FROM) * AHEAD // span, (m - MAX_FROM + 1) * AHEAD // span)


def blocks_at(step):
    def before(step):
        groups, rest = divmod(step, 2 * TILES)
        return min(AHEAD + groups * sum(BLOCKS_PER_STEP) + sum(BLOCKS_PER_STEP[:rest]), GROUPS * NMAX)
    return range(before(step), before(step + 1))


def score_bank(s):
    s = s % (2 * TILES * GROUPS)
    return SCORE_BANK + 2 * (s % 2) if s < THREE_PAIRS_FROM else \
        (SCORE_BANK, SCORE_BANK + 2, MAX_BANK)[(s - THREE_PAIRS_FROM) % 3]


def up_bank(m):
    ring = 3 if m < MAX_FROM - 1 else 2
    return (UP_BANK, UP_BANK + 1, MAX_BANK)[m % ring]


class Place:

    def __init__(self, turn, hold, links=(0, 0)):
        self.turn = turn
        self.hold = hold
        self.chunk = hold(turn * (2 * FFN_CHUNKS) + FFN_CHUNKS)
        self.unit = hold(turn * (2 * EXPERTS) + EXPERTS)
        self.ffn = hold(turn * 2 + 1)
        self.added = hold(turn * (2 * (EXPERTS - 1)) + (EXPERTS - 1))
        self.att = hold(turn * 1)
        self.groups = hold(turn * GROUPS)
        self.tiles = hold(turn * (GROUPS * TILES))
        self.scores = hold(turn * (2 * GROUPS * TILES))
        self.maxes = hold(turn * (GROUPS * NMAX))
        self.misc = hold(turn * len(MISC_TURN) + len(MISC_FIRST))
        self.next_att = hold(turn * 1 + 1)
        self.next_stacks = hold(turn * 2 + 2)
        self.next_groups = hold((turn + 1) * GROUPS)
        self.next_tiles = hold((turn + 1) * (GROUPS * TILES))
        self.next_scores = hold((turn + 1) * (2 * GROUPS * TILES))
        self.stats = hold(turn * 3 + 2)
        self.next_maxes = hold(turn * (GROUPS * NMAX) + GROUPS * NMAX)
        self.nth = {"0": 0, "1": 1, "a": 2}
        self.links = hold(turn * links[1] + links[0])
        self.first_kind = 0
        self.names = MISC_TURN
        self.at = AT


class Coming:

    def __init__(self, p):
        self.groups, self.tiles, self.scores, self.maxes = p.next_groups, p.next_tiles, p.next_scores, p.next_maxes
        self.misc, self.names = p.misc, p.names


class First(Place):

    def __init__(self):
        self.turn = -1
        self.chunk = self.unit = self.ffn = self.added = self.att = self.groups = 0
        self.tiles = self.scores = self.maxes = self.misc = self.stats = self.links = 0
        self.first_kind = 0
        self.next_att = self.next_stacks = self.next_maxes = self.next_groups = self.next_tiles = self.next_scores = 0
        self.nth = {"0": 0, "a": 1}
        self.names = MISC_FIRST
        self.at = AT_FIRST


class Last(Place):

    def __init__(self, links=(0, 0)):
        super().__init__(TURNS, lambda value: value, links)
        self.first_kind = 1
        self.nth = {"1": 0}
        self.names = MISC_LAST
        self.at = AT_LAST


POOL_LINKS = (7, 9)
DVE_LINKS = (51, 99)


CONST_LOADS = 15


def counted(found, stated, name):
    assert found == stated, f"{name}: {found}, not {stated}"


def build(nc, x, wq, wk, wv, wo, gamma, beta, Wg, W1, b1, W2, b2,
          ident_d, mask_d, maskT_d, rope_d, rank_d, pick_d, out):
    with ExitStack() as ctx:
        def sb(name, shape, dt=F32):
            return ctx.enter_context(nc.sbuf_tensor(name, shape, dt))

        def sem(name):
            return ctx.enter_context(nc.semaphore(name))

        psum = ctx.enter_context(nc.psum_tensor("psum", [P, 8, 512], F32))

        ident = sb("ident", [P, P])
        ident16 = sb("ident16", [P, P], BF16)
        mask_f = sb("mask_f", [P, 2, P])
        mask16 = sb("mask16", [P, 2, KV, P], BF16)
        rope = sb("rope", [P, TILES, 2, HALF])
        spare = sb("spare", [P, 1])
        warm = sb("warm", [P, 1])
        rank = sb("rank", [P, EXPERTS])
        pick_f = sb("pick_f", [2 * EXPERTS, EXPERTS, P])
        pick = sb("pick", [2 * EXPERTS, EXPERTS, P], F32R)
        power = sb("power", [P, 2, TILES])
        euler = sb("euler", [P, EXPERTS])
        small = sb("small", [50, P])
        smallT = sb("smallT", [P, 50])
        w1_hi = sb("w1_hi", [P, EXPERTS, F], F32R)
        w1_lo = sb("w1_lo", [P, EXPERTS, F], F32R)
        w2_hi = sb("w2_hi", [P, EXPERTS, CHUNKS, D], F32R)
        w2_lo = sb("w2_lo", [P, EXPERTS, CHUNKS, D], F32R)
        wqkv = sb("wqkv", [P, QKV])
        wo_s = sb("wo_s", [P, D])
        b1T = smallT[:, 0:32]
        b2T = smallT[:, 32:40]
        WgT = smallT[:, 40:48]
        gammaT = smallT[:, 48:49]
        betaT = smallT[:, 49:50]
        x_in = sb("x_in", [P, TILES, D])
        x1 = sb("x1", [P, TILES, D])
        x2 = sb("x2", [P, TILES, D])
        x_out = sb("x_out", [P, TILES, D])
        stats = sb("stats", [P, TILES, 6])
        mv = sb("mv", [P, TILES, 2])
        vt = sb("vt", [P, 6, TILES])
        rt = sb("rt", [P, 3, TILES])
        constant = sb("constant", [P, 2, TILES])
        res = [sb(f"res{k}", [P, TILES, D]) for k in range(2)]
        xn = sb("xn", [P, S])
        xn_hi = [sb(f"xn_hi{k}", [P, S], F32R) for k in range(2)]
        xn_lo = [sb(f"xn_lo{k}", [P, S], F32R) for k in range(2)]
        gs = sb("gs", [P, 10, TILES, EXPERTS])
        gr = sb("gr", [P, 8, TILES])
        gaug = sb("gaug", [P, TILES, 2 * EXPERTS])
        gT = [sb(f"gT{k}", [2 * EXPERTS, S], F32R) for k in range(2)]
        h = sb("h", [P, CHUNKS, S])
        h_hi = sb("h_hi", [P, CHUNKS, S], F32R)
        h_lo = sb("h_lo", [P, CHUNKS, S], F32R)
        gate = sb("gate", [P, 2, S])
        part = sb("part", [P, 2, S])
        acc = [sb(f"acc{k}", [P, S]) for k in range(2)]
        qk = sb("qk", [P, TILES, QK])
        turned = sb("turned", [P, 4, TILES, ROPED, HALF])
        rot = sb("rot", [P, TILES, ROPED, HD])
        aug = sb("aug", [P, TILES, ROPED, SLOT])
        v = sb("v", [P, TILES, KV, SLOT])
        kT = sb("kT", [P, KV, S], F32R)
        qT = sb("qT", [P, GROUPS, S], F32R)
        q2T = sb("q2T", [P, 2, S], F32R)
        negmax = sb("negmax", [P, TILES, HEADS])
        probs = sb("probs", [P, 2, KV, S])
        arrived = probs[:].rearrange("p a h s -> p (a h) s")

        def w1_f(e):
            return arrived[:, 2 * (e % 4)]

        def w2_f(e):
            return arrived[:, 2 * (e % 4) + 1]

        u = sb("u", [P, S])
        rden = sb("rden", [P, TILES, KV])
        ao = sb("ao", [P, TILES, D])
        z = na = turned[:, 0:2].rearrange("p a i h c -> p (a i h c)")[:, 0:TILES * D]\
            .rearrange("p (i d) -> p i d", i=TILES)
        nT = aoT = u

        const_loaded = sem("const_loaded")
        expert_loaded = [sem(f"expert_loaded{e}") for e in range(EXPERTS)]
        x_loaded = sem("x_loaded")
        x_out_free = sem("x_out_free")
        ones_set = sem("ones_set")
        consts_cast = sem("consts_cast")
        small_turned = sem("small_turned")
        small_ready = sem("small_ready")
        w_hi_ready = sem("w_hi_ready")
        w_lo_ready = sem("w_lo_ready")
        dve_link = sem("dve_link")
        pool_link = sem("pool_link")
        stats_ready = sem("stats_ready")
        scale_ready = sem("scale_ready")
        z_ready = sem("z_ready")
        res_ready = sem("res_ready")
        xn_ready = sem("xn_ready")
        gates_ready = sem("gates_ready")
        n_ready = sem("n_ready")
        rotated = sem("rotated")
        aug_ready = sem("aug_ready")
        misc_full = sem("misc_full")
        misc_taken = sem("misc_taken")
        gate_exp = sem("gate_exp")
        up_done = sem("up_done")
        down_done = sem("down_done")
        gate_spread = sem("gate_spread")
        gate_copied = sem("gate_copied")
        gelu_done = sem("gelu_done")
        split_done = sem("split_done")
        scaled = sem("scaled")
        added = sem("added")
        max_full = sem("max_full")
        max_taken = sem("max_taken")
        max_split = sem("max_split")
        scores_full = sem("scores_full")
        exp_done = sem("exp_done")
        pv_done = sem("pv_done")
        u_copied = sem("u_copied")

        block = ctx.enter_context(nc.Block())

        def misc(n=512):
            return psum[:, MISC_BANK, 0:n]

        def misc_at(p, name):
            return p.misc + p.names.index(name)

        def wait(eng, s, value):
            if not isinstance(value, int) or value > 0:
                eng.wait_ge(s, value)

        def hooks(steps, m, p):
            for name, step in steps.items():
                if p.at.get(name) == m:
                    step(p)

        def spreads(p, m):
            return m % CHUNKS == SPREAD and not (m < CHUNKS and "spread" in p.at)

        def heads_of(t, g):
            return t[:, :, g * KV:(g + 1) * KV, :]

        @block.sync
        def _(sp):
            def load(seq):
                sp.dma_start(x_in[:], x[seq].rearrange("(i p) d -> p i d", p=P)).then_inc(x_loaded, 16)

            def store(seq):
                sp.dma_start(out[seq].rearrange("(i p) d -> p i d", p=P), x_out[:]).then_inc(x_out_free, 16)

            load(0)
            for dst, src in ((small[0:32], b1.rearrange("e (c p) -> (e c) p", p=P)), (small[32:40], b2),
                             (small[40:48], Wg), (small[48:49], gamma[None, :]),
                             (small[49:50], beta[None, :]), (rank[:], rank_d), (pick_f[:], pick_d)):
                sp.dma_start(dst, src).then_inc(const_loaded, 16)
            for e in range(EXPERTS):
                if e >= 4:
                    sp.wait_ge(w_lo_ready, 2 * (e - 3))
                sp.dma_start(w1_f(e), W1[e]).then_inc(expert_loaded[e], 16)
                sp.dma_start(w2_f(e).rearrange("p (c d) -> p c d", c=CHUNKS),
                             W2[e].rearrange("(c p) d -> p c d", p=P)).then_inc(expert_loaded[e], 16)
            sp.wait_ge(z_ready, 1)
            sp.wait_ge(res_ready, 1)
            load(1)
            with sp.Fori(0, TURNS - 1) as turn:
                p = Place(turn, sp.snap)
                sp.wait_ge(z_ready, p.ffn + 1)
                sp.wait_ge(res_ready, p.ffn + 1)
                load(turn + 2)
                sp.wait_ge(misc_taken, misc_at(p, "fin:1") + 1)
                store(turn)
            p = Place(TURNS - 1, int)
            sp.wait_ge(misc_taken, misc_at(p, "fin:1") + 1)
            store(TURNS - 1)
            p = Last()
            sp.wait_ge(misc_taken, misc_at(p, "fin:1") + 1)
            store(TURNS)
            sp.wait_ge(x_out_free, 16 + 16 * SEQS)

        @block.gpsimd
        def _(pool):
            at = [0]
            base = [0]

            def link(ins):
                at[0] += 1
                ins.then_inc(pool_link, 1)
                pool.wait_ge(pool_link, base[0] + at[0])

            def norm_scale(p, nth):
                pool.wait_ge(stats_ready, p.stats + p.nth[nth] + 1)
                if nth == "a":
                    r = pool.tensor_tensor(vt[:, 2], vt[:, 0], power[:, 0], ALU.pow)
                else:
                    link(pool.tensor_tensor(vt[:, 2:4], vt[:, 0:2], power[:], ALU.pow))
                    r = pool.tensor_tensor(vt[:, 5], vt[:, 2], vt[:, 3], ALU.mult)
                r.then_inc(scale_ready, 1)

            def make_res(p, k, src):
                half_r, factor, shift = [rt[:, n] for n in range(3)]
                pool.wait_ge(scale_ready, p.stats + p.nth[str(k)] + 1)
                link(pool.tensor_tensor(half_r, vt[:, 2], constant[:, 0], ALU.mult))
                pool.tensor_tensor(factor, half_r, constant[:, 1], ALU.add)
                link(pool.tensor_tensor(shift, half_r, mv[:, :, 0], ALU.mult))
                link(pool.tensor_tensor(res[k][:], src[:], factor[:, :, None].broadcast_to([P, TILES, D]), ALU.mult))
                pool.tensor_tensor(res[k][:], res[k][:], shift[:, :, None].broadcast_to([P, TILES, D]),
                                   ALU.subtract).then_inc(res_ready, 1)

            def rotate(p):
                pool.wait_ge(misc_taken, misc_at(p, "qkv1") + 1)
                t = qk[:].rearrange("p i (h a c) -> p i h a c", a=2, c=HALF)
                for n in range(2):
                    cs = rope[:, :, n, None, :].broadcast_to([P, TILES, ROPED, HALF])
                    ins = pool.tensor_tensor(turned[:, n], t[:, :, :, n, :], cs, ALU.mult)
                link(ins)
                pool.tensor_tensor(rot[:, :, :, 0:HALF], turned[:, 0], turned[:, 1], ALU.subtract)\
                    .then_inc(rotated, 1)

            def add(p, n):
                k, e = n // EXPERTS, n % EXPERTS
                if e == 0:
                    return
                sums = p.added + (EXPERTS - 1) * k
                total = acc[k + p.first_kind]
                pool.wait_ge(scaled, p.unit + n + 1)
                if e == 1:
                    pool.tensor_tensor(total[:], part[:, 0], part[:, 1], ALU.add).then_inc(added, 1)
                else:
                    wait(pool, added, sums + (e - 1))
                    pool.tensor_tensor(total[:], total[:], part[:, e % 2], ALU.add).then_inc(added, 1)

            def ffns(p, count, steps):
                for m in range(count * FFN_CHUNKS):
                    if m >= LAG and (m - LAG) % CHUNKS == CHUNKS - 1:
                        add(p, (m - LAG) // CHUNKS)
                    hooks(steps, m, p)
                add(p, count * EXPERTS - 1)

            def exp_gate(p):
                pool.wait_ge(misc_taken, misc_at(p, "logits:1") + 1)
                pool.tensor_tensor(gs[:, 1], euler[:, None, :].broadcast_to([P, TILES, EXPERTS]), gs[:, 0],
                                   ALU.pow).then_inc(gate_exp, 1)

            pool.memset(x_out[:], 0.0).then_inc(x_out_free, 16)
            pool.memset(euler[:], float(np.e))
            pool.memset(constant[:, 0], 0.5)
            pool.memset(constant[:, 1], 1.0)
            link(pool.memset(power[:], -0.5))
            p = First()
            norm_scale(p, "0")
            make_res(p, 0, x_in)
            pool.memset(kT[:].bitcast(F32), 0.0)
            pool.memset(aug[:], 0.0)
            link(pool.memset(v[:], 0.0))
            pool.memset(aug[:, :, HEADS:ROPED, STACK:STACK + 2], 1.0)
            pool.memset(v[:, :, :, HD:HD + 1], 1.0).then_inc(ones_set, 1)
            ffns(p, 1, {})
            norm_scale(p, "a")
            rotate(p)
            counted(at[0], POOL_LINKS[0], "POOL_LINKS, first")
            with pool.Fori(0, TURNS) as turn:
                p = Place(turn, pool.snap, POOL_LINKS)
                at[0], base[0] = 0, p.links
                norm_scale(p, "0")
                make_res(p, 0, x_in)
                ffns(p, 2, {"stats:1": lambda p: norm_scale(p, "1"), "res:1": lambda p: make_res(p, 1, x2),
                            "gate_exp:1": exp_gate,
                            "stats:a": lambda p: norm_scale(p, "a"), "rope": rotate})
                counted(at[0], POOL_LINKS[1], "POOL_LINKS, turn")
            p = Last(POOL_LINKS)
            at[0], base[0] = 0, p.links
            norm_scale(p, "1")
            make_res(p, 1, x2)
            exp_gate(p)
            ffns(p, 1, {})

        @block.scalar
        def _(act):
            for dst, src in ((ident[:], ident_d), (mask_f[:, 0], mask_d), (mask_f[:, 1], maskT_d),
                             (rope[:], rope_d), (wqkv[:, 0:D], wq), (wqkv[:, D:D + KV * HD], wk),
                             (wqkv[:, QK:QKV], wv), (wo_s[:], wo)):
                act.dma_start(dst, src).then_inc(const_loaded, 16)
            act.wait_ge(small_turned, 1)
            act.activation(smallT[:], misc(50), ACT.Copy).then_inc(small_ready, 1)
            act.wait_ge(small_ready, 1)

            def weights_hi(e, halves=(0, 1)):
                act.wait_ge(expert_loaded[e], 32)
                if 0 in halves:
                    act.activation(w1_hi[:, e], w1_f(e), ACT.Copy).then_inc(w_hi_ready, 1)
                if 1 in halves:
                    act.activation(w2_hi[:, e].rearrange("p c d -> p (c d)"), w2_f(e), ACT.Copy)\
                       .then_inc(w_hi_ready, 1)

            def take(p, name, *pairs):
                act.wait_ge(misc_full, misc_at(p, name) + 1)
                for dst, src in pairs:
                    ins = act.activation(dst, src, ACT.Copy)
                ins.then_inc(misc_taken, 1)

            def take_z(p):
                act.wait_ge(misc_full, misc_at(p, "zT:1") + 1)
                wait(act, xn_ready, p.ffn + (1 - p.first_kind))
                act.activation(xn[:], misc(), ACT.Identity, bias=betaT, scale=gammaT)
                act.activation(xn_hi[1][:], misc(), ACT.Identity, bias=betaT, scale=gammaT)\
                   .then_inc(misc_taken, 1)

            def exp_gate(p):
                act.wait_ge(misc_taken, misc_at(p, "logits:0") + 1)
                act.activation(gs[:, 1], gs[:, 0], ACT.Exp).then_inc(gate_exp, 1)

            def take_gates(p, k):
                take(p, f"gT:{k}", (gT[k][:], psum[0:2 * EXPERTS, MISC_BANK, :]))

            def take_qkv(p, half):
                src = misc(2 * QKV).rearrange("p (i c) -> p i c", i=2)
                t = slice(2 * half, 2 * half + 2)
                act.wait_ge(misc_full, misc_at(p, f"qkv{half}") + 1)
                for i in range(2):
                    act.activation(v[:, 2 * half + i, :, 0:HD],
                                   src[:, i, QK:QKV].rearrange("p (h d) -> p h d", h=KV), ACT.Copy)
                act.activation(qk[:, t], src[:, :, 0:QK], ACT.Copy).then_inc(misc_taken, 1)

            def gelu(p, m):
                e, c = m // CHUNKS % EXPERTS, m % CHUNKS
                act.wait_ge(up_done, p.chunk + m + 1)
                wait(act, split_done, p.chunk + (m - CHUNKS + 1))
                bias = b1T[:, CHUNKS * e + c:CHUNKS * e + c + 1]
                if c % 2:
                    wait(act, down_done, p.chunk + (m - CHUNKS + 1))
                    act.activation(h_hi[:, c], psum[:, up_bank(m)], ACT.Gelu_apprx_tanh, bias=bias)
                act.activation(h[:, c], psum[:, up_bank(m)], ACT.Gelu_apprx_tanh, bias=bias)\
                   .then_inc(gelu_done, 1)

            def copy_gate(p, n):
                act.wait_ge(gate_spread, p.unit + n + 1)
                wait(act, scaled, p.unit + (n - 1))
                act.activation(gate[:, n % 2], psum[:, GATE_BANK], ACT.Copy).then_inc(gate_copied, 1)

            def ffns(p, count, steps, first=False):
                for m in range(count * FFN_CHUNKS):
                    gelu(p, m)
                    if first and m % 2 == 0 and m // CHUNKS + 2 < EXPERTS:
                        weights_hi(m // CHUNKS + 2, (m % CHUNKS // 2,))
                    if spreads(p, m):
                        copy_gate(p, m // CHUNKS)
                    hooks(steps, m, p)

            def copy_u(p, g):
                act.wait_ge(pv_done, p.tiles + TILES * (g + 1))
                if g > 0:
                    act.wait_ge(misc_full, misc_at(p, f"uT{g - 1}") + 1)
                act.activation(u[:], psum[:, PV_BANK], ACT.Copy).then_inc(u_copied, 1)

            def take_q2(p, g):
                take(p, f"q2T{g}", (q2T[:, g % 2], misc()))

            def take_o(p):
                take(p, "aT", (aoT[:], misc()))

            def exp_scores(p, s):
                tile, pair = s // 2, s % 2
                j, n, b = tile % TILES, S - P * (tile % TILES), score_bank(s)
                act.wait_ge(scores_full, p.scores + s + 1)
                if tile >= 2:
                    wait(act, pv_done, p.tiles + (tile - 1))
                act.activation(probs[:, j % 2, 2 * pair:2 * pair + 2, 0:n],
                               psum[:, b:b + 2, 0:n], ACT.Exp, scale=SCALE).then_inc(exp_done, 1)

            def attend(p, prepares):
                for s in range(HEAD_STEPS, 2 * TILES * GROUPS):
                    g, j = s // (2 * TILES), s // 2 % TILES
                    exp_scores(p, s)
                    if s == 24 and prepares:
                        exp_gate(p)
                    if s % 2 == 0:
                        continue
                    if j == 0 and g == 1:
                        copy_u(p, 0)
                    if g < GROUPS - 2 and j == 2:
                        take_q2(p, g + 1)
                if prepares:
                    act.activation(warm[:], smallT[:, 0:1], ACT.Gelu_apprx_tanh)
                    take_gates(p, 0)
                copy_u(p, GROUPS - 1)

            def begin(p):
                for s in range(HEAD_STEPS):
                    exp_scores(Coming(p), s)

            after = {"nT": lambda p: take(p, "nT", (nT[:], misc())),
                     "qkv0": lambda p: take_qkv(p, 0), "qkv1": lambda p: take_qkv(p, 1),
                     "kT": lambda p: take(p, "kT", *[(kT[SLOT * kv:SLOT * (kv + 1), kv],
                                                      psum[SLOT * kv:SLOT * (kv + 1), MISC_BANK, :])
                                                     for kv in range(KV)])}
            for g in range(GROUPS):
                after[f"qT{g}"] = lambda p, g=g: take(p, f"qT{g}", (qT[:, g], misc()))
            after["q2T0"] = lambda p: take_q2(p, 0)
            between = {"aT": take_o, "zT:1": take_z}
            gates = {k: {f"gT:{k}": lambda p, k=k: take_gates(p, k)} for k in range(2)}
            spread = {"spread": lambda p: copy_gate(p, 0)}

            p = First()
            weights_hi(0)
            weights_hi(1)
            exp_gate(p)
            ffns(p, 1, gates[0] | spread, first=True)
            act.wait_ge(ones_set, 1)
            for step in after.values():
                step(p)
            begin(p)
            with act.Fori(0, TURNS) as turn:
                p = Place(turn, act.snap)
                attend(p, True)
                ffns(p, 2, between | gates[1] | after)
                begin(p)
            p = Last()
            attend(p, False)
            for step in between.values():
                step(p)
            ffns(p, 1, gates[1] | spread)

        @block.vector
        def _(dve):
            at = [0]
            base = [0]

            def link(ins):
                at[0] += 1
                ins.then_inc(dve_link, 1)
                dve.wait_ge(dve_link, base[0] + at[0])

            def along(col, n):
                return col[:, :, None].broadcast_to([P, TILES, n])

            def weights_lo(e, half):
                dve.wait_ge(w_hi_ready, 2 * e + half + 1)
                if half == 0:
                    dve.tensor_tensor(w1_lo[:, e], w1_f(e), w1_hi[:, e].bitcast(F32), ALU.subtract)\
                       .then_inc(w_lo_ready, 1)
                else:
                    dve.tensor_tensor(w2_lo[:, e].rearrange("p c d -> p (c d)"), w2_f(e),
                                      w2_hi[:, e].rearrange("p c d -> p (c d)").bitcast(F32), ALU.subtract)\
                       .then_inc(w_lo_ready, 1)

            def statistics(src, twice):
                for i in range(TILES):
                    ins = dve.bn_stats(stats[:, i], src[:, i])
                link(ins)
                dve.memset(spare[:], 0.0)
                for i in range(TILES):
                    ins = dve.bn_aggr(mv[:, i], stats[:, i])
                link(ins)
                ins = dve.tensor_scalar(vt[:, 0], mv[:, :, 1], EPS, None, ALU.add)
                if twice:
                    link(ins)
                    link(dve.reciprocal(vt[:, 4], vt[:, 0]))
                    link(dve.tensor_tensor(vt[:, 4], mv[:, :, 1], vt[:, 4], ALU.mult))
                    ins = dve.tensor_scalar(vt[:, 1], vt[:, 4], EPS, None, ALU.add)
                ins.then_inc(stats_ready, 1)

            def normalize(dst, src, scale, tiles=range(TILES)):
                for i in tiles:
                    ins = dve.tensor_scalar(dst[:, i], src[:, i], mv[:, i, 0:1], scale[:, i:i + 1],
                                            ALU.subtract, ALU.mult)
                return ins

            def make_z(p, k, src, tiles=range(TILES)):
                if tiles[0] == 0:
                    dve.wait_ge(scale_ready, p.stats + p.nth[str(k)] + 1)
                ins = normalize(z, src, vt[:, 5], tiles)
                if tiles[-1] == TILES - 1:
                    ins.then_inc(z_ready, 1)

            def make_xn(p):
                dve.wait_ge(misc_full, misc_at(p, "zT:0") + 1)
                ins = dve.tensor_scalar(xn[:], misc(), gammaT, betaT, ALU.mult, ALU.add)
                ins.then_inc(misc_taken, 1)
                dve.wait_ge(misc_taken, misc_at(p, "zT:0") + 1)
                link(dve.tensor_copy(xn_hi[0][:], xn[:]))

            def make_xlo(p, k):
                if k == 0:
                    make_xn(p)
                else:
                    dve.wait_ge(misc_taken, misc_at(p, "zT:1") + 1)
                dve.tensor_tensor(xn_lo[k][:], xn[:], xn_hi[k][:].bitcast(F32), ALU.subtract)\
                   .then_inc(xn_ready, 1)

            def shift_logits(p, k):
                dve.wait_ge(misc_full, misc_at(p, f"logits:{k}") + 1)
                logits = misc(TILES * EXPERTS).rearrange("p (i e) -> p i e", i=TILES)
                link(dve.tensor_reduce(gr[:, 0], logits, AX_X, ALU.max))
                dve.tensor_tensor(gs[:, 0], logits, along(gr[:, 0], EXPERTS), ALU.subtract)\
                   .then_inc(misc_taken, 1)

            def make_gates(p, k):
                _, ex, pr, eq, one1, left, one2, both, share, ranked = [gs[:, n] for n in range(10)]
                top0, total, inverse, top1, top2, best, sum2, inverse2 = [gr[:, n] for n in range(8)]
                ranks = rank[:, None, :].broadcast_to([P, TILES, EXPERTS])
                hi = gaug[:, :, 0:EXPERTS]

                def pick_largest(values, top, one):
                    yield lambda: dve.tensor_reduce(top, values, AX_X, ALU.max)
                    yield lambda: dve.tensor_tensor(eq, values, along(top, EXPERTS), ALU.is_equal)
                    yield lambda: dve.tensor_tensor(ranked, eq, ranks, ALU.mult)
                    yield lambda: dve.tensor_reduce(best, ranked, AX_X, ALU.max)
                    yield lambda: dve.tensor_tensor(one, ranks, along(best, EXPERTS), ALU.is_equal)

                yield lambda: dve.tensor_reduce(total, ex, AX_X, ALU.add)
                yield lambda: dve.reciprocal(inverse, total)
                yield lambda: dve.tensor_tensor(pr, ex, along(inverse, EXPERTS), ALU.mult)
                yield from pick_largest(pr, top1, one1)
                yield lambda: dve.scalar_tensor_tensor(left, one1, -2.0, pr, ALU.mult, ALU.add)
                yield from pick_largest(left, top2, one2)
                yield lambda: dve.scalar_tensor_tensor(sum2, top1, GATE_EPS, top2, ALU.add, ALU.add)
                yield lambda: dve.reciprocal(inverse2, sum2)
                yield lambda: dve.tensor_tensor(both, one1, one2, ALU.add)
                yield lambda: dve.tensor_tensor(both, both, pr, ALU.mult)
                yield lambda: dve.tensor_tensor(share, both, along(inverse2, EXPERTS), ALU.mult)
                yield lambda: dve.tensor_copy(hi.bitcast(F32R), share)
                yield lambda: dve.tensor_tensor(gaug[:, :, EXPERTS:2 * EXPERTS], share, hi, ALU.subtract)

            def gate_steps(p, k):
                reached = None
                steps = list(make_gates(p, k))
                for n, step in enumerate(steps):
                    if reached is None:
                        dve.wait_ge(gate_exp, p.ffn + (k - p.first_kind) + 1)
                    else:
                        dve.wait_ge(dve_link, reached)
                    if n < len(steps) - 1:
                        at[0] += 1
                        reached = base[0] + at[0]
                        step().then_inc(dve_link, 1)
                    else:
                        step().then_inc(gates_ready, 1)
                    yield

            def round_h(p, m):
                c = m % CHUNKS
                dve.wait_ge(gelu_done, p.chunk + m + 1)
                wait(dve, down_done, p.chunk + (m - CHUNKS + 1))
                at[0] += 1
                dve.tensor_copy(h_hi[:, c], h[:, c]).then_inc(dve_link, 1)
                return base[0] + at[0]

            def rest_h(p, m, rounded=None):
                c = m % CHUNKS
                if rounded is None:
                    dve.wait_ge(gelu_done, p.chunk + m + 1)
                    wait(dve, down_done, p.chunk + (m - CHUNKS + 1))
                else:
                    dve.wait_ge(dve_link, rounded)
                dve.tensor_tensor(h_lo[:, c], h[:, c], h_hi[:, c].bitcast(F32), ALU.subtract)\
                   .then_inc(split_done, 1)

            def scale(p, n):
                e = n % EXPERTS
                sums = p.added + (EXPERTS - 1) * (n // EXPERTS)
                dve.wait_ge(down_done, p.chunk + CHUNKS * (n + 1))
                dve.wait_ge(gate_copied, p.unit + n + 1)
                wait(dve, added, sums + (max(e - 2, 1) if e > 1 else 0))
                dve.scalar_tensor_tensor(part[:, e % 2], psum[:, Y_BANK + n % 2], b2T[:, e:e + 1],
                                         gate[:, n % 2], ALU.add, ALU.mult).then_inc(scaled, 1)

            def ffns(p, count, steps, first=False, gating=None):
                gating = gating or gate_steps(p, 1)
                rounded = None

                def tick(n=1):
                    if m >= (GATES_FROM if count == 2 else 0 if first else 1):
                        for _ in range(n):
                            next(gating, None)

                for m in range(count * FFN_CHUNKS):
                    blocks = list(blocks_after(m))
                    if m % 2 == 0:
                        rounded = round_h(p, m)
                        tick()
                        take_maxes(p, blocks[:1])
                        if m > 0:
                            rest_h(p, m - 1)
                        tick()
                        if not blocks:
                            rest_h(p, m, rounded)
                            rounded = None
                    else:
                        if rounded is not None:
                            rest_h(p, m - 1, rounded)
                        take_maxes(p, blocks[:1])
                    tick()
                    if m == count * FFN_CHUNKS - 1:
                        rest_h(p, m)
                    take_maxes(p, blocks[1:])
                    if m >= LAG and (m - LAG) % CHUNKS == CHUNKS - 1:
                        scale(p, (m - LAG) // CHUNKS)
                    hooks(steps, m, p)
                    tick(1 if count == 2 else 3 if first else 5)
                    if first and m % 2 == 1 and m // CHUNKS + 2 < EXPERTS:
                        weights_lo(m // CHUNKS + 2, m % CHUNKS // 2)
                scale(p, count * EXPERTS - 1)

            def finish(p, k, dst):
                dve.wait_ge(misc_full, misc_at(p, f"fin:{k}") + 1)
                dve.wait_ge(res_ready, p.ffn + (k - p.first_kind) + 1)
                if k == 1:
                    wait(dve, x_out_free, p.turn * 16 + 16)
                ins = dve.scalar_tensor_tensor(dst[:].rearrange("p i d -> p (i d)"), misc(), 0.5,
                                               res[k][:].rearrange("p i d -> p (i d)"), ALU.mult, ALU.add)
                ins.then_inc(misc_taken, 1)
                dve.wait_ge(misc_taken, misc_at(p, f"fin:{k}") + 1)

            def norm_for_attention(p):
                dve.wait_ge(scale_ready, p.stats + p.nth["a"] + 1)
                normalize(na, x1, vt[:, 2]).then_inc(n_ready, 1)

            def rotate(p):
                dve.wait_ge(misc_taken, misc_at(p, "qkv1") + 1)
                t = qk[:].rearrange("p i (h a c) -> p i h a c", a=2, c=HALF)
                for n in range(2):
                    cs = rope[:, :, 1 - n, None, :].broadcast_to([P, TILES, ROPED, HALF])
                    ins = dve.tensor_tensor(turned[:, 2 + n], t[:, :, :, n, :], cs, ALU.mult)
                link(ins)
                link(dve.tensor_tensor(rot[:, :, :, HALF:HD], turned[:, 2], turned[:, 3], ALU.add))

            def stack(p, keys):
                dve.wait_ge(rotated, p.next_att + 1)
                h0, h1, his, lo = (HEADS, ROPED, (0, 2 * HD), HD) if keys else (0, HEADS, (0, HD), 2 * HD)
                for a in his:
                    ins = dve.tensor_copy(aug[:, :, h0:h1, a:a + HD].bitcast(F32R), rot[:, :, h0:h1])
                if not keys:
                    dve.memset(aug[:, :, 0:HEADS, STACK:STACK + 2], 0.0)
                link(ins)
                dve.tensor_tensor(aug[:, :, h0:h1, lo:lo + HD], rot[:, :, h0:h1],
                                  aug[:, :, h0:h1, 0:HD], ALU.subtract).then_inc(aug_ready, 1)

            def take_max(maxes, at):
                g, (tile, heads) = at // NMAX, MAX_BLOCKS[at % NMAX]
                n, h0 = P * (tile + 1), g * KV + heads[0]
                dve.wait_ge(max_full, maxes + at + 1)
                src = psum[:, MAX_BANK + at % 2, 0:n * len(heads)].rearrange("p (h n) -> p h n", n=n)
                dve.tensor_reduce(negmax[:, tile, h0:h0 + len(heads)], src, AX_X, ALU.max, negate=True)\
                   .then_inc(max_taken, 1)

            def take_maxes(p, blocks):
                for block in blocks:
                    take_max(p.next_maxes, block)

            def split_max(p, g):
                dve.wait_ge(max_taken, p.maxes + NMAX * (g + 1))
                heads = slice(g * KV, (g + 1) * KV)
                src = negmax[:, :, heads, None]
                hi = heads_of(aug, g)[:, :, :, STACK:STACK + 1]
                link(dve.tensor_copy(hi.bitcast(F32R), src))
                dve.tensor_tensor(heads_of(aug, g)[:, :, :, STACK + 1:STACK + 2], src, hi, ALU.subtract)\
                   .then_inc(max_split, 1)

            def copy_u(p, g):
                dve.wait_ge(pv_done, p.tiles + TILES * (g + 1))
                dve.wait_ge(misc_full, misc_at(p, f"uT{g - 1}") + 1)
                dve.tensor_copy(u[:], psum[:, PV_BANK]).then_inc(u_copied, 1)

            def divide(p, g):
                dve.wait_ge(misc_full, misc_at(p, f"uT{g}") + 1)
                src = misc().rearrange("p (i h c) -> p i h c", i=TILES, h=KV)
                link(dve.reciprocal(rden[:], src[:, :, :, HD]))
                dst = ao[:].rearrange("p i (g h d) -> p i g h d", g=GROUPS, h=KV)[:, :, g]
                dve.tensor_tensor(dst, src[:, :, :, 0:HD],
                                  rden[:, :, :, None].broadcast_to([P, TILES, KV, HD]), ALU.mult)\
                   .then_inc(misc_taken, 1)

            def attend(p, prepares):
                if prepares:
                    gating = gate_steps(p, 0)
                for step in range(HEAD_STEPS, 2 * TILES * GROUPS):
                    g = step // (2 * TILES)
                    if step % (2 * TILES) == 4 and g > 0:
                        divide(p, g - 1)
                    for block in blocks_at(step):
                        take_max(p.maxes, block)
                        if (block + 1) % NMAX == 0:
                            split_max(p, block // NMAX)
                    if step == 5 and prepares:
                        dve.wait_ge(x_loaded, (p.turn + 2) * 16)
                        statistics(x_in, True)
                    if step in (10, 11) and prepares:
                        make_z(p, 0, x_in, range(2 * step - 20, 2 * step - 18))
                    if step % (2 * TILES) == 1 and g > 1:
                        copy_u(p, g - 1)
                    if step == 21:
                        dve.wait_ge(misc_full, misc_at(p, "q2T3") + 1)
                        dve.tensor_copy(q2T[:, 3 % 2], misc()).then_inc(misc_taken, 1)
                    if step == 18 and prepares:
                        make_xlo(p, 0)
                    if step == 23 and prepares:
                        shift_logits(p, 0)
                    if step >= 25 and prepares:
                        for _ in range(4):
                            next(gating, None)
                if prepares:
                    assert next(gating, "all") == "all"

            def begin(p):
                split_max(Coming(p), 1)
                for step in range(HEAD_STEPS):
                    take_maxes(p, blocks_at(step))

            def add_attention(p):
                dve.wait_ge(misc_full, misc_at(p, "y") + 1)
                dve.tensor_tensor(x2[:].rearrange("p i d -> p (i d)"), misc(),
                                  x1[:].rearrange("p i d -> p (i d)"), ALU.add).then_inc(misc_taken, 1)
                dve.wait_ge(misc_taken, misc_at(p, "y") + 1)

            def again(p):
                if not isinstance(p, Last):
                    dve.wait_ge(res_ready, p.ffn + 1)
                statistics(x2, True)

            between = {"norm3": lambda p: divide(p, GROUPS - 1), "y": add_attention,
                       "stats:1": again, "z:1": lambda p: make_z(p, 1, x2),
                       "xlo:1": lambda p: make_xlo(p, 1)}
            logits = {"logits:1": lambda p: shift_logits(p, 1)}
            after = {"fin:0": lambda p: finish(p, 0, x1), "stats:a": lambda p: statistics(x1, False),
                     "n:a": norm_for_attention, "rotate": rotate,
                     "stackK": lambda p: stack(p, True), "stackQ": lambda p: stack(p, False)}
            first_max = {"max0": lambda p: split_max(Coming(p), 0)}

            p = First()
            dve.wait_ge(x_loaded, 16)
            statistics(x_in, True)
            make_z(p, 0, x_in)
            dve.wait_ge(small_ready, 1)
            make_xlo(p, 0)
            shift_logits(p, 0)
            weights_lo(0, 0)
            weights_lo(0, 1)
            dve.tensor_copy(ident16[:], ident[:])
            gating = gate_steps(p, 0)
            for kv in range(KV):
                next(gating)
                dve.tensor_copy(mask16[:, :, kv], mask_f[:])
            next(gating)
            dve.tensor_copy(pick[:], pick_f[:]).then_inc(consts_cast, 1)
            next(gating)
            weights_lo(1, 0)
            next(gating)
            weights_lo(1, 1)
            ffns(p, 1, {}, first=True, gating=gating)
            for step in after.values():
                step(p)
            take_maxes(p, range(NMAX))
            split_max(Coming(p), 0)
            take_maxes(p, range(NMAX, AHEAD))
            begin(p)
            counted(at[0], DVE_LINKS[0], "DVE_LINKS, first")
            with dve.Fori(0, TURNS) as turn:
                p = Place(turn, dve.snap, DVE_LINKS)
                at[0], base[0] = 0, p.links
                attend(p, True)
                ffns(p, 2, between | logits | after | first_max)
                begin(p)
                finish(p, 1, x_out)
                counted(at[0], DVE_LINKS[1], "DVE_LINKS, turn")
            p = Last(DVE_LINKS)
            at[0], base[0] = 0, p.links
            attend(p, False)
            for step in between.values():
                step(p)
            ffns(p, 1, logits)
            finish(p, 1, x_out)

        @block.tensor
        def _(pe):
            mm = nc.tensor.matmul

            def use_misc(p, name):
                wait(pe, misc_taken, misc_at(p, name))

            def turn_tiles(p, name, parts, rows=P):
                use_misc(p, name)
                for i, part_i in enumerate(parts):
                    ins = nc.tensor.transpose(psum[0:rows, MISC_BANK, i * P:(i + 1) * P], part_i, ident[:])
                ins.then_inc(misc_full, 1)

            def turn_z(p, k):
                pe.wait_ge(z_ready, p.ffn + (k - p.first_kind) + 1)
                turn_tiles(p, f"zT:{k}", [z[:, i] for i in range(TILES)])

            def make_logits(p, k, tiles=range(TILES)):
                use_misc(p, f"logits:{k}")
                for i in tiles:
                    ins = mm(psum[:, MISC_BANK, i * EXPERTS:(i + 1) * EXPERTS], xn[:, i * P:(i + 1) * P],
                             WgT, start=True, stop=True)
                if tiles[-1] == TILES - 1:
                    ins.then_inc(misc_full, 1)

            def turn_gates(p, k):
                pe.wait_ge(gates_ready, p.ffn + (k - p.first_kind) + 1)
                turn_tiles(p, f"gT:{k}", [gaug[:, i] for i in range(TILES)], 2 * EXPERTS)

            def up(p, m, first):
                n, e, c = m // CHUNKS, m // CHUNKS % EXPERTS, m % CHUNKS
                k = n // EXPERTS + p.first_kind
                if m % FFN_CHUNKS == 0:
                    pe.wait_ge(xn_ready, p.ffn + (k - p.first_kind) + 1)
                if first and c == 0:
                    pe.wait_ge(w_lo_ready, 2 * (e + 1))
                if m == 0 and not isinstance(p, First):
                    pe.wait_ge(exp_done, p.scores + 2 * GROUPS * TILES - 1)
                if m == 2 and not isinstance(p, First):
                    pe.wait_ge(max_taken, p.maxes + GROUPS * NMAX)
                ahead = 2 if m < MAX_FROM - 1 else 1
                wait(pe, gelu_done, p.chunk + (m - ahead))
                o, cols = psum[:, up_bank(m)], slice(c * P, (c + 1) * P)
                mm(o, w1_hi[:, e, cols], xn_hi[k][:], start=True, stop=False)
                mm(o, w1_hi[:, e, cols], xn_lo[k][:], start=False, stop=False)
                mm(o, w1_lo[:, e, cols], xn_hi[k][:], start=False, stop=True).then_inc(up_done, 1)
                if spreads(p, m):
                    spread(p, n)

            def spread(p, n):
                k, e = n // EXPERTS + p.first_kind, n % EXPERTS
                wait(pe, gate_copied, p.unit + n)
                if e == 0:
                    pe.wait_ge(misc_taken, misc_at(p, f"gT:{k}") + 1)
                if isinstance(p, First):
                    pe.wait_ge(consts_cast, 1)
                if n == 0 and not isinstance(p, First):
                    pe.wait_ge(u_copied, p.groups + GROUPS)
                mm(psum[:, GATE_BANK], pick[:, e], gT[k][:], start=True, stop=True).then_inc(gate_spread, 1)

            def down(p, m):
                n, e, c = m // CHUNKS, m // CHUNKS % EXPERTS, m % CHUNKS
                pe.wait_ge(split_done, p.chunk + m + 1)
                if c == 0:
                    wait(pe, scaled, p.unit + (n - 1))
                o = psum[:, Y_BANK + n % 2]
                mm(o, w2_hi[:, e, c], h_hi[:, c], start=(c == 0), stop=False)
                mm(o, w2_hi[:, e, c], h_lo[:, c], start=False, stop=False)
                mm(o, w2_lo[:, e, c], h_hi[:, c], start=False, stop=(c == CHUNKS - 1)).then_inc(down_done, 1)

            def ffns(p, count, steps, first=False, tail=None):
                for m in range(count * FFN_CHUNKS):
                    blocks = list(blocks_after(m))
                    up(p, m, first)
                    block_maxes(p, blocks[:1])
                    if m >= LAG:
                        if m == LAG and not isinstance(p, First):
                            pe.wait_ge(exp_done, p.scores + 2 * GROUPS * TILES)
                        down(p, m - LAG)
                    block_maxes(p, blocks[1:])
                    hooks(steps, m, p)
                for m in range(count * FFN_CHUNKS - LAG, count * FFN_CHUNKS):
                    if tail is not None and m == count * FFN_CHUNKS - 1:
                        tail(p)
                    down(p, m)

            def finish(p, k):
                pe.wait_ge(added, p.added + (EXPERTS - 1) * (k - p.first_kind + 1))
                turn_tiles(p, f"fin:{k}", [acc[k][:, i * P:(i + 1) * P] for i in range(TILES)])

            def turn_n(p):
                pe.wait_ge(n_ready, p.next_att + 1)
                turn_tiles(p, "nT", [na[:, i] for i in range(TILES)])

            def project(p, half):
                use_misc(p, f"qkv{half}")
                for i in range(2):
                    t = 2 * half + i
                    ins = mm(psum[:, MISC_BANK, i * QKV:(i + 1) * QKV], nT[:, t * P:(t + 1) * P], wqkv[:],
                             start=True, stop=True)
                ins.then_inc(misc_full, 1)

            def turn_heads(p, name, h0):
                turn_tiles(p, name, [aug[:, i, h0:h0 + KV].rearrange("p h c -> p (h c)")
                                     for i in range(TILES)])

            def turn_keys(p):
                pe.wait_ge(aug_ready, p.next_stacks + 1)
                turn_heads(p, "kT", HEADS)

            def turn_queries(p, g):
                if g == 0:
                    pe.wait_ge(aug_ready, p.next_stacks + 2)
                turn_heads(p, f"qT{g}", g * KV)

            def block_max(maxes, at):
                g, (tile, heads) = at // NMAX, MAX_BLOCKS[at % NMAX]
                n = P * (tile + 1)
                if at >= 2:
                    wait(pe, max_taken, maxes + (at - 1))
                o = psum[:, MAX_BANK + at % 2, 0:n * len(heads)].rearrange("p (h n) -> p h n", n=n)
                mm(o, qT[:, g, tile * P:(tile + 1) * P], kT[:, heads[0]:heads[-1] + 1, 0:n], start=True, stop=False)
                mm(o[:, :, tile * P:n], ident16[:], mask16[:, 0, 0:len(heads)], start=False, stop=True)\
                    .then_inc(max_full, 1)

            def block_maxes(p, blocks):
                for at in blocks:
                    if at % NMAX == 0:
                        pe.wait_ge(misc_taken, misc_at(p, f"qT{at // NMAX}") + 1)
                    if at < 2:
                        wait(pe, gelu_done, p.chunk + (FFN_CHUNKS if isinstance(p, First) else MAX_FROM - 1))
                    block_max(p.next_maxes, at)

            def turn_q2(p, g):
                pe.wait_ge(max_split, p.groups + g + 1)
                turn_heads(p, f"q2T{g}", g * KV)

            def score(p, g, j, pair):
                s, n = 2 * (TILES * g + j) + pair, S - P * j
                if s == THREE_PAIRS_FROM + 2:
                    pe.wait_ge(max_taken, p.maxes + GROUPS * NMAX)
                if s >= 2:
                    wait(pe, exp_done, p.scores + (s - 1 - (s > THREE_PAIRS_FROM + 2)))
                if s % (2 * TILES) == 0:
                    pe.wait_ge(misc_taken, misc_at(p, f"q2T{g}") + 1)
                bank = score_bank(s)
                for i in range(2):
                    mm(psum[:, bank + i, 0:n], kT[:, 2 * pair + i, j * P:(j + 1) * P],
                       q2T[:, g % 2, j * P:S], start=True, stop=False)
                for i in range(2):
                    ins = mm(psum[:, bank + i, 0:P], ident16[:], mask16[:, 1, 0], start=False, stop=True)
                ins.then_inc(scores_full, 1)

            def weigh(p, g, j):
                pe.wait_ge(exp_done, p.scores + 2 * (TILES * g + j + 1))
                if j == 0 and g > 0:
                    wait(pe, u_copied, p.groups + g)
                for kv in range(KV):
                    ins = mm(psum[SLOT * kv:SLOT * (kv + 1), PV_BANK, j * P:S], v[:, j, kv],
                             probs[:, j % 2, kv, 0:S - P * j], start=(j == 0), stop=(j == TILES - 1))
                ins.then_inc(pv_done, 1)

            def turn_u(p, g):
                pe.wait_ge(u_copied, p.groups + g + 1)
                turn_tiles(p, f"uT{g}", [u[:, i * P:(i + 1) * P] for i in range(TILES)])

            def turn_o(p):
                turn_tiles(p, "aT", [ao[:, i] for i in range(TILES)])

            def project_o(p):
                use_misc(p, "y")
                for i in range(TILES):
                    ins = mm(psum[:, MISC_BANK, i * D:(i + 1) * D], aoT[:, i * P:(i + 1) * P], wo_s[:],
                             start=True, stop=True)
                ins.then_inc(misc_full, 1)

            def score_step(p, step):
                score(p, step // (2 * TILES), step // 2 % TILES, step % 2)
                for block in blocks_at(step):
                    block_max(p.maxes, block)

            def score_first(p):
                pe.wait_ge(gelu_done, p.chunk + ffn_count(p) * FFN_CHUNKS)
                score(Coming(p), 0, 0, 0)

            def begin(p):
                for block in blocks_at(0):
                    block_max(p.next_maxes, block)
                pe.wait_ge(scaled, p.unit + ffn_count(p) * EXPERTS)
                pe.wait_ge(gate_copied, p.unit + ffn_count(p) * EXPERTS)
                for step in range(1, HEAD_STEPS):
                    score_step(Coming(p), step)
                weigh(Coming(p), 0, 0)

            def ffn_count(p):
                return 1 if isinstance(p, First) else 2

            def attend(p, prepares):
                for step in range(HEAD_STEPS, 2 * TILES * GROUPS):
                    g, j = step // (2 * TILES), step // 2 % TILES
                    if step == 16 and prepares:
                        turn_z(p, 0)
                    score_step(p, step)
                    if step in (22, 23) and prepares:
                        make_logits(p, 0, range(2 * step - 44, 2 * step - 42))
                    if step % 2 == 0:
                        continue
                    if g < GROUPS - 1 and j == 2:
                        turn_q2(p, g + 1)
                    if j > 0:
                        weigh(p, g, j - 1)
                    elif g > 0:
                        weigh(p, g - 1, TILES - 1)
                    if j == 1 and g > 0:
                        turn_u(p, g - 1)
                if prepares:
                    turn_gates(p, 0)
                weigh(p, GROUPS - 1, TILES - 1)

            between = {"uT3": lambda p: turn_u(p, GROUPS - 1), "aT": turn_o, "y": project_o,
                       "zT:1": lambda p: turn_z(p, 1)}
            gates = {"logits:1": lambda p: make_logits(p, 1), "gT:1": lambda p: turn_gates(p, 1)}
            late = {"spread": lambda p: spread(p, 0)}
            after = {"fin:0": lambda p: finish(p, 0), "nT": turn_n, "qkv0": lambda p: project(p, 0),
                     "qkv1": lambda p: project(p, 1), "kT": turn_keys}
            for g in range(GROUPS):
                after[f"qT{g}"] = lambda p, g=g: turn_queries(p, g)
            start_queries = {"q2T0": lambda p: turn_q2(Coming(p), 0)}

            pe.wait_ge(const_loaded, 16 * CONST_LOADS)
            nc.tensor.transpose(misc(50), small[:], ident[0:50, 0:50]).then_inc(small_turned, 1)
            pe.wait_ge(small_ready, 1)
            p = First()
            turn_z(p, 0)
            make_logits(p, 0)
            ffns(p, 1, {"gT:0": lambda p: turn_gates(p, 0)} | late, first=True)
            done = 0
            for name, step in after.items():
                step(p)
                if name in ("qT0", "qT1", "qT2"):
                    block_maxes(p, range(done, done + 3))
                    done += 3
            block_maxes(p, range(done, AHEAD))
            turn_q2(Coming(p), 0)
            score_first(p)
            begin(p)
            with pe.Fori(0, TURNS) as turn:
                p = Place(turn, pe.snap)
                attend(p, True)
                ffns(p, 2, between | gates | after | start_queries, tail=score_first)
                begin(p)
                finish(p, 1)
            p = Last()
            attend(p, False)
            for step in between.values():
                step(p)
            ffns(p, 1, gates | late)
            finish(p, 1)


NAMES = ["L0_attn_x", "L0_attn_wq", "L0_attn_wk", "L0_attn_wv", "L0_attn_wo", "L0_ffn_gamma",
         "L0_ffn_beta", "L0_ffn_Wg", "L0_ffn_W1", "L0_ffn_b1", "L0_ffn_W2", "L0_ffn_b2"]


def shape_constants():
    f = np.float32
    at = np.arange(P)
    inverse = f(1.0) / f(10000.0) ** (np.arange(HALF, dtype=f) / f(HALF))
    angle = np.arange(S, dtype=f)[:, None] * inverse[None, :]
    rope = np.stack([np.cos(angle), np.sin(angle)], axis=1).astype(f)
    rope = rope.reshape(TILES, P, 2, HALF).transpose(1, 0, 2, 3)
    rank = np.broadcast_to(np.arange(EXPERTS, 0, -1).astype(f), (P, EXPERTS))
    pick = np.zeros((2 * EXPERTS, EXPERTS, P), f)
    for row in range(2 * EXPERTS):
        pick[row, row % EXPERTS] = 1.0
    return {"table_identity": np.eye(P, dtype=f),
            "table_mask": np.where(at[None, :] <= at[:, None], f(0.0), f(MASKED)),
            "table_mask_turned": np.where(at[None, :] >= at[:, None], f(0.0), f(MASKED)),
            "table_rope": rope, "table_rank": rank, "table_pick": pick}


def kernel(**inputs):
    import concourse.bacc as bacc
    from concourse.bass_utils import run_bass_kernel_spmd

    nc = bacc.Bacc("TRN2", target_bir_lowering=False, num_devices=1)
    arrays = {name: np.ascontiguousarray(inputs[name]) for name in NAMES}
    arrays.update({name: np.ascontiguousarray(a) for name, a in shape_constants().items()})
    args = [nc.dram_tensor(name, a.shape, mybir.dt.from_np(a.dtype), kind="ExternalInput").ap()
            for name, a in arrays.items()]
    out = nc.dram_tensor("out", (SEQS, S, D), F32, kind="ExternalOutput").ap()
    build(nc, *args, out)
    return run_bass_kernel_spmd(nc, [arrays], core_ids=[0]).results[0]["out"]
```
